# Optimizing a Trainium2 kernel written in Bass

```python
import numpy as np
import jax
import jax.numpy as jnp

def _softmax(x, axis=-1):
    return jax.nn.softmax(x, axis=axis)

def _gelu(x):
    return jax.nn.gelu(x, approximate=True)

def _silu(x):
    return jax.nn.silu(x)

def _sigmoid(x):
    return jax.nn.sigmoid(x)

def _layernorm(x, axis=-1, eps=1e-05):
    m = jnp.mean(x, axis=axis, keepdims=True)
    v = jnp.var(x, axis=axis, keepdims=True)
    return (x - m) / jnp.sqrt(v + eps)

def _scatter_add(tgt, idx, src, axis=0):
    return tgt.at[idx].add(src)

def _segment_sum(src, seg, n):
    return jax.ops.segment_sum(src, seg, n)
kernel_name = 'mk_seq_postln_d1_jaxref_r8_fb465f'

def setup_inputs(seed: int=0):
    np.random.seed(seed)
    _w = jnp.asarray

    def _L0_attn_setup():
        import jax, jax.numpy as jnp
        import numpy as np
        HEADS = 16
        DIM_HEAD = 64
        HEIGHT = 16
        KERNEL = 5
        DILATION = 1
        ALPHA = 32 ** 2

        def stable_softmax(t, axis=-1, alpha=ALPHA):
            t = t / alpha
            t = t - jax.lax.stop_gradient(jnp.max(t, axis=axis, keepdims=True))
            return jax.nn.softmax(t * alpha, axis=axis)
        key = jax.random.key(seed)
        ks = jax.random.split(key, 5)
        b, n, dim = (4, 4097, 128)
        inner = HEADS * DIM_HEAD
        x = jax.random.normal(ks[0], (b, n, dim), dtype=jnp.float32)
        w_qkv = jax.random.normal(ks[1], (dim, 3 * inner), dtype=jnp.float32) * dim ** (-0.5)
        w_out = jax.random.normal(ks[2], (inner, dim), dtype=jnp.float32) * inner ** (-0.5)
        b_out = jax.random.normal(ks[3], (dim,), dtype=jnp.float32) * 0.02
        w_th = jax.random.normal(ks[4], (HEADS, HEADS), dtype=jnp.float32) * HEADS ** (-0.5)
        return {'x': x, 'w_qkv': w_qkv, 'w_out': w_out, 'b_out': b_out, 'w_th': w_th}
    _L0_attn_in = _L0_attn_setup()

    def _L0_ffn_setup():
        import jax, jax.numpy as jnp
        import numpy as np
        EPS = 1e-08

        def _ternary_linear(x, w):
            alpha = jnp.mean(jnp.abs(w))
            w_t = jnp.sign(w) * (jnp.abs(w) > 0.5 * alpha).astype(w.dtype)
            w_q = w + jax.lax.stop_gradient(w_t - w)
            d = x.shape[-1]
            rms = jnp.sqrt(jnp.sum(x * x, axis=-1, keepdims=True)) / jnp.sqrt(jnp.asarray(d, x.dtype))
            x_norm = x / (rms + EPS)
            return jnp.einsum('bsd,fd->bsf', x_norm, w_q)
        key = jax.random.key(seed)
        k1, k2, k3 = jax.random.split(key, 3)
        d_model, d_ff = (128, 512)
        B, S = (4, 512)
        x = jax.random.normal(k1, (B, S, d_model), dtype=jnp.float32)
        w_up = jax.random.normal(k2, (d_ff, d_model), dtype=jnp.float32) * 0.02
        w_down = jax.random.normal(k3, (d_model, d_ff), dtype=jnp.float32) * 0.02
        return {'x': x, 'w_up': w_up, 'w_down': w_down}
    _L0_ffn_in = _L0_ffn_setup()
    _d = {'L0_attn_x': _L0_attn_in['x'], 'L0_attn_w_qkv': _L0_attn_in['w_qkv'], 'L0_attn_w_out': _L0_attn_in['w_out'], 'L0_attn_b_out': _L0_attn_in['b_out'], 'L0_attn_w_th': _L0_attn_in['w_th'], 'L0_ffn_w_up': _L0_ffn_in['w_up'], 'L0_ffn_w_down': _L0_ffn_in['w_down']}
    _x0 = _d['L0_attn_x']
    _d['L0_attn_x'] = jax.random.normal(jax.random.fold_in(jax.random.key(seed), 1), (2, 1024, 128), dtype=_x0.dtype)
    del _x0
    return _d

def reference(L0_attn_x, L0_attn_w_qkv, L0_attn_w_out, L0_attn_b_out, L0_attn_w_th, L0_ffn_w_up, L0_ffn_w_down):

    def _L0_attn_ref(x, w_qkv, w_out, b_out, w_th):
        import jax, jax.numpy as jnp
        import numpy as np
        HEADS = 16
        DIM_HEAD = 64
        HEIGHT = 16
        KERNEL = 5
        DILATION = 1
        ALPHA = 32 ** 2

        def stable_softmax(t, axis=-1, alpha=ALPHA):
            t = t / alpha
            t = t - jax.lax.stop_gradient(jnp.max(t, axis=axis, keepdims=True))
            return jax.nn.softmax(t * alpha, axis=axis)
        b, n, dim = x.shape
        h, d = (HEADS, DIM_HEAD)
        height, K, dil = (HEIGHT, KERNEL, DILATION)
        pad = dil * (K - 1) // 2
        scale = d ** (-0.5)
        kernel_numel = K * height
        seq_pad = -(n - 1) % height
        xp = jnp.pad(x, ((0, 0), (0, seq_pad), (0, 0))) if seq_pad > 0 else x
        qkv = xp @ w_qkv
        q, k, v = jnp.split(qkv, 3, axis=-1)
        if n == 1:
            return v @ w_out + b_out
        out_bos = v[:, :1]

        def to_heads(t):
            return t.reshape(b, -1, h, d).transpose(0, 2, 1, 3)
        q, k, v = map(to_heads, (q, k, v))
        q = q * scale
        k_bos, k = (k[:, :, 0], k[:, :, 1:])
        v_bos, v = (v[:, :, 0], v[:, :, 1:])
        q = q[:, :, 1:]
        X = q.shape[2] // height
        k = k.reshape(b, h, X, height, d)
        v = v.reshape(b, h, X, height, d)
        kp = jnp.pad(k, ((0, 0), (0, 0), (pad, pad), (0, 0), (0, 0)))
        vp = jnp.pad(v, ((0, 0), (0, 0), (pad, pad), (0, 0), (0, 0)))
        idx = jnp.arange(X)[:, None] + jnp.arange(K)[None, :] * dil
        kw = kp[:, :, idx].reshape(b, h, X, kernel_numel, d)
        vw = vp[:, :, idx].reshape(b, h, X, kernel_numel, d)
        kb = jnp.broadcast_to(k_bos[:, :, None, None, :], (b, h, X, 1, d))
        vb = jnp.broadcast_to(v_bos[:, :, None, None, :], (b, h, X, 1, d))
        kw = jnp.concatenate([kb, kw], axis=3)
        vw = jnp.concatenate([vb, vw], axis=3)
        qw = q.reshape(b, h, X, height, d)
        sim = jnp.einsum('bhnid,bhnjd->bhnij', qw, kw)
        seq_len = X * height
        q_range = jnp.arange(seq_len).reshape(X, height)
        k_range = jnp.pad(jnp.arange(seq_len).reshape(X, height), ((pad, pad), (0, 0)), constant_values=seq_len)
        kr = k_range[idx].reshape(X, kernel_numel)
        mask = q_range[:, :, None] < kr[:, None, :]
        mask = jnp.pad(mask, ((0, 0), (0, 0), (1, 0)), constant_values=False)
        mask_value = -jnp.finfo(sim.dtype).max
        sim = jnp.where(mask[None, None], mask_value, sim)
        attn = stable_softmax(sim, axis=-1)
        attn = jnp.einsum('gh,bhnij->bgnij', w_th, attn)
        out = jnp.einsum('bhnij,bhnjd->bhnid', attn, vw)
        out = out.transpose(0, 2, 3, 1, 4).reshape(b, X * height, h * d)
        out = jnp.concatenate([out_bos, out], axis=1)
        return (out @ w_out + b_out)[:, :n]

    def _L0_ffn_ref(x, w_up, w_down):
        import jax, jax.numpy as jnp
        import numpy as np
        EPS = 1e-08

        def _ternary_linear(x, w):
            alpha = jnp.mean(jnp.abs(w))
            w_t = jnp.sign(w) * (jnp.abs(w) > 0.5 * alpha).astype(w.dtype)
            w_q = w + jax.lax.stop_gradient(w_t - w)
            d = x.shape[-1]
            rms = jnp.sqrt(jnp.sum(x * x, axis=-1, keepdims=True)) / jnp.sqrt(jnp.asarray(d, x.dtype))
            x_norm = x / (rms + EPS)
            return jnp.einsum('bsd,fd->bsf', x_norm, w_q)
        h = jax.nn.gelu(_ternary_linear(x, w_up), approximate=False)
        return _ternary_linear(h, w_down)
    x = L0_attn_x
    x = _layernorm(x + _L0_attn_ref(x, L0_attn_w_qkv, L0_attn_w_out, L0_attn_b_out, L0_attn_w_th), axis=-1)
    x = _layernorm(x + _L0_ffn_ref(x, L0_ffn_w_up, L0_ffn_w_down), axis=-1)
    return x

_drawn_inputs = setup_inputs


def setup_inputs(seed=0):
    import zlib

    import numpy as np

    out = dict(_drawn_inputs(seed))
    spreads = {}
    factors = {'L0_attn_b_out': 2.782}
    for name, (base, spread) in spreads.items():
        noise = np.random.default_rng([zlib.crc32(name.encode()), seed]).standard_normal(out[name].shape)
        drawn = base * np.exp(spread * noise) if base else spread * noise
        out[name] = jnp.asarray(drawn.astype(out[name].dtype))
    for name, factor in factors.items():
        out[name] = (out[name] * factor).astype(out[name].dtype)
    return out
```

```python
import concourse.bass as bass
from concourse import mybir
from contextlib import ExitStack, nullcontext

F32 = mybir.dt.float32
F32R = mybir.dt.float32r
BF16 = mybir.dt.bfloat16
ALU = mybir.AluOpType
ACT = mybir.ActivationFunctionType
AX = mybir.AxisListType
RADD = bass.bass_isa.ReduceOp.add

B, N, D = 2, 1024, 128
H, DH = 16, 64
INNER = H * DH
FF = 512
P = 128
BLK = 16
SEG = BLK + 1
WIN = 3 * SEG - 1
PITCH = 64
IL = 8
ITER_TOK = 512
ITERS = B * N // ITER_TOK
IBLK = ITER_TOK // BLK
CHUNK = 256
CBLK = CHUNK // BLK
CPAIR = CBLK // 2
STEP_BLK = 4
SLOTS = IBLK // STEP_BLK
TILES = 2 * STEP_BLK
NEG = -float(2.0 ** 100)
XCOLS = (IBLK + 2) * SEG
LEAD = 2 * BLK
XROWS = LEAD + ITER_TOK
SCALE = float(DH) ** -0.5
EPS_LN, EPS_RMS = 1e-5, 1e-8
TPI = ITER_TOK // P
NT = B * N // P
FT = FF // P
CONSTS = (-0.5, 0.5, EPS_LN, 1.0 / D, 1.0 / FF)
MINUS_HALF, HALF, EPS, PER_D, PER_FF = range(5)


def attention_ffn(nc, x, w_qkv, w_out, b_out, w_th, w_up, w_down, out, x_rows, bos_rows, pt_rows):
    ctx = ExitStack()
    with ctx:
        def sb(name, shape, dt=F32):
            return ctx.enter_context(nc.sbuf_tensor(name, shape, dt))

        def sem(name):
            return ctx.enter_context(nc.semaphore(name))

        ident = sb("ident", [P, P])
        sel = sb("sel", [P, P], BF16)
        mask = sb("mask", [P, 2, TILES * WIN], BF16)
        sel8 = sb("sel8", [P, IL])
        wth8 = sb("wth8", [P, H])
        kron = sb("kron", [P, P])
        zrow = sb("zrow", [LEAD, P])
        tsum = sb("tsum", [P, 8])
        v0T = sb("v0T", [P, 8 * B])
        consts = sb("consts", [P, len(CONSTS), TPI])
        b_sb = sb("b_sb", [P, 1])
        Gh = sb("Gh", [P, H, P], F32R)
        Gl = sb("Gl", [P, H, P], F32R)
        Mh = sb("Mh", [P, H, P], F32R)
        Ml = sb("Ml", [P, H, P], F32R)
        bosT = sb("bosT", [P, B])
        wuT = sb("wuT", [P, FF], F32R)
        wdT = sb("wdT", [P, FT, P])
        xq = sb("xq", [P, NT, P])
        xTh = sb("xTh", [P, B * N], F32R)
        xTl = sb("xTl", [P, B * N], F32R)
        xT17 = sb("xT17", [P, ITERS, IBLK + 2, SEG])
        xw = [[sb(f"xw{i}{s}", [P, CPAIR, P], F32R) for s in "hl"] for i in range(2)]
        attnT = sb("attnT", [P, B * N])

        with ExitStack() as prep:
            def pb(name, shape, dt=F32):
                return prep.enter_context(nc.sbuf_tensor(name, shape, dt))

            w_sb = pb("w_sb", [P, 3 * INNER])
            wT = pb("wT", [P, 24, P])
            wo_sb = pb("wo_sb", [P, 8, P])
            PT = pb("PT", [P, H, P])
            R = pb("R", [P, H, P])
            xqh = pb("xqh", [P, NT, P], F32R)
            xql = pb("xql", [P, NT, P], F32R)
            w_ff = pb("w_ff", [P, 2, FF])
            tern = pb("tern", [P, 2, FF])
        with ExitStack() as attention:
            def ab(name, shape, dt=F32):
                return attention.enter_context(nc.sbuf_tensor(name, shape, dt))

            CTh = [ab(f"CTh{i}", [P, H, CHUNK], F32R) for i in range(2)]
            CTl = [ab(f"CTl{i}", [P, H, CHUNK], F32R) for i in range(2)]
            ATh = [ab(f"ATh{i}", [P, 512], F32R) for i in range(2)]
            ATl = [ab(f"ATl{i}", [P, 512], F32R) for i in range(2)]
            Yb = [ab(f"Yb{i}", [P, CHUNK // IL, P]) for i in range(2)]
            E = [ab(f"E{i}", [P, TILES, PITCH]) for i in range(2)]
            mx = [ab(f"mx{i}", [P, TILES]) for i in range(2)]
            sm = [ab(f"sm{i}", [P, TILES]) for i in range(2)]
            rc = [ab(f"rc{i}", [P, TILES]) for i in range(2)]
        attnS = sb("attnS", [P, ITER_TOK])
        res = sb("res", [P, TPI, P])
        x1 = sb("x1", [P, TPI, P])
        xn = sb("xn", [P, TPI, P])
        sq = sb("sq", [P, FF])
        xnTh = sb("xnTh", [P, ITER_TOK], F32R)
        xnTl = sb("xnTl", [P, ITER_TOK], F32R)
        gS = [sb(f"gS{i}", [P, FF]) for i in range(2)]
        hT = [sb(f"hT{i}", [P, FT, P]) for i in range(2)]
        y2 = sb("y2", [P, TPI, P])
        outS = sb("outS", [P, NT, P])
        st = sb("st", [P, TPI, 6])
        mv = sb("mv", [P, TPI, 2])
        st2 = sb("st2", [P, TPI, 6])
        mv2 = sb("mv2", [P, TPI, 2])
        ssq = sb("ssq", [P, TPI])
        rms = sb("rms", [P, TPI])
        inv = sb("inv", [P, TPI])
        hss = sb("hss", [P, TPI])
        hrms = sb("hrms", [P, TPI])
        hinv = sb("hinv", [P, TPI])
        rstd = sb("rstd", [P, TPI])
        rstd2 = sb("rstd2", [P, TPI])
        vpe = sb("vpe", [P, TPI])
        vpe2 = sb("vpe2", [P, TPI])

        bank = [ctx.enter_context(nc.psum_tensor(f"bank{i}", [P, 512], F32)) for i in range(8)]
        S_BANK, Y_BANK, T_BANK, C_BANK, O_BANK = [0, 1], [2, 3], 4, [5, 6], 7

        s_xq, s_wqkv, s_wout, s_small, s_wff = map(sem, ("s_xq", "s_wqkv", "s_wout", "s_small", "s_wff"))
        s_ident, s_pool, s_const, s_sel8, s_kron, s_zero, s_epad = map(sem, (
            "s_ident", "s_pool", "s_const", "s_sel8", "s_kron", "s_zero", "s_epad"))
        s_fill, s_eva, s_evd = map(sem, ("s_fill", "s_evac_act", "s_evac_dve"))
        s_xqh, s_xql, s_xrows, s_pt, s_R = map(sem, ("s_xqh", "s_xql", "s_xrows", "s_pt", "s_R"))
        s_asum, s_atot, s_thr, s_ternd, s_tern = map(sem, ("s_asum", "s_atot", "s_thr", "s_ternd", "s_tern"))
        s_mask, s_sel = sem("s_mask"), sem("s_sel")
        MASKS = 1 + 2 * 4 + 2
        s_win = [sem("s_win0"), sem("s_win1")]
        s_Y, s_Ye = sem("s_Y"), sem("s_Ye")
        s_S, s_max, s_sub, s_exp, s_sum, s_rec, s_norm = map(sem, (
            "s_S", "s_max", "s_sub", "s_exp", "s_sum", "s_rec", "s_norm"))
        s_T, s_ATh, s_ATl = map(sem, ("s_T", "s_ATh", "s_ATl"))
        s_C, s_CTh, s_CTl = map(sem, ("s_C", "s_CTh", "s_CTl"))
        s_O, s_Oe = sem("s_O"), sem("s_Oe")
        f_stage, f_aT, f_res, f_st, f_var, f_rstd, f_x1, f_ssq, f_rms, f_inv, f_xn = map(sem, (
            "f_stage", "f_aT", "f_res", "f_st", "f_var", "f_rstd", "f_x1", "f_ssq", "f_rms", "f_inv", "f_xn"))
        f_xT, f_xTh, f_xTl, f_up, f_gelu, f_hT, f_hTe, f_sq, f_hrms, f_hinv, f_dn = map(sem, (
            "f_xT", "f_xTh", "f_xTl", "f_up", "f_gelu", "f_hT", "f_hTe", "f_sq", "f_hrms", "f_hinv", "f_dn"))
        f_y2, f_st2, f_var2, f_rstd2, f_out, f_store = map(sem, (
            "f_y2", "f_st2", "f_var2", "f_rstd2", "f_out", "f_store"))
        f_seen = sem("f_seen")
        s_bos, f_bosput, f_eps, f_eps2, f_r1, f_h1 = map(sem, ("s_bos", "f_bosput", "f_eps", "f_eps2", "f_r1", "f_h1"))

        FILLS = ([("x", i, i, "AD") for i in range(4)]
                 + [("w", i, (4, 5, 6, 7, 0, 1)[i], "A" if i % 2 == 0 else "D") for i in range(4)]
                 + [("g", i, i, "AD") for i in range(4)]
                 + [("w", i, (4, 5)[i - 4], "A" if i % 2 == 0 else "D") for i in (4, 5)]
                 + [("p", i, (6, 7, 0, 1)[i], "A" if i % 2 == 0 else "D") for i in range(4)])
        TAIL = ([("m", i, (4, 5, 6, 7)[i], "AD") for i in range(4)]
                + [("t", 0, 0, "A"), ("t", 1, 1, "D"), ("v0", 0, 4, "D"), ("bos", 0, 5, "D")])
        ALLF = FILLS + TAIL

        def fill_no(kind, i):
            return next(n for n, f in enumerate(ALLF) if f[:2] == (kind, i)) + 1

        def read_no(who, kind, i):
            return sum(who in f[3] for f in ALLF[:fill_no(kind, i)])

        def bank_free(eng, kind, i):
            n = fill_no(kind, i) - 1
            for before in reversed(ALLF[:n]):
                if before[2] == ALLF[n][2]:
                    if "A" in before[3]:
                        eng.wait_ge(s_eva, read_no("A", *before[:2]))
                    if "D" in before[3]:
                        eng.wait_ge(s_evd, read_no("D", *before[:2]))
                    return

        WDMAS = 2 * (2 * 3 + 2 * 2)

        AHEAD_SUB = AHEAD_ATL = AHEAD_O = AHEAD_OE = 1
        AHEAD_C, AHEAD_CT = 8, 4

        def since(eng, I, j, d):
            return nullcontext() if j >= d else eng.If(I > 0)

        def before_last(eng, I, j):
            return nullcontext() if j < SLOTS // 2 else eng.If(I < ITERS - 1)

        def heads(i):
            return [8 * (i // 2) + i % 2 + 2 * k for k in range(4)]

        def Y_out(b, chunk_par, h0):
            return Yb[chunk_par][:, :, IL * h0:IL * h0 + 2 * IL].rearrange("p t (h i) -> p h t i", i=IL)

        def ct_view(buf, sc, q):
            v = buf[:, :, :].rearrange("p h (r q s) -> p h r q s", q=2, s=BLK)
            return v[:, :, 2 * sc:2 * sc + 2, q, :].rearrange("p h r s -> p r h s")

        def c_view(bk):
            return bank[C_BANK[bk]][:, :].rearrange("p (r h s) -> p r h s", r=2, s=BLK)

        def f32(ap):
            return ap.bitcast(F32)

        block = ctx.enter_context(nc.Block())

        @block.sync
        def _(sp):
            for b in range(B):
                t0 = b * (NT // B)
                sp.dma_start(xq[:, t0:t0 + 7, :], x[b, 1:897, :].rearrange("(m p) c -> p m c", p=P)).then_inc(s_xq, 16)
                sp.dma_start(xq[0:127, t0 + 7, :], x[b, 897:1024, :]).then_inc(s_xq, 16)
                sp.dma_start(xq[127:128, t0 + 7, :], x[b, 0:1, :]).then_inc(s_xq, 16)
            sp.dma_start(wo_sb[:, :, :], w_out.rearrange("(t p) n -> p t n", p=P)).then_inc(s_wout, 16)
            sp.wait_ge(s_zero, 1)
            for hl in range(2):
                for it in (0, 2):
                    sp.dma_start(x_rows[hl][it, 0:LEAD, :], zrow[:, :]).then_inc(s_xrows, 16)
            for hl, src, ready in ((0, xqh, s_xqh), (1, xql, s_xql)):
                sp.wait_ge(ready, 1)
                for it in range(ITERS):
                    sp.dma_start(x_rows[hl][it, LEAD:XROWS, :].rearrange("(m p) c -> p m c", p=P),
                                 f32(src[:, TPI * it:TPI * it + TPI, :])).then_inc(s_xrows, 16)
                    last = (it // 2 + 1) * (NT // B) - 1
                    sp.dma_start(bos_rows[hl][it:it + 1, :], f32(src[127:128, last, :])).then_inc(s_xrows, 16)
                for it in (1, 3):
                    sp.dma_start(x_rows[hl][it, 0:LEAD, :], f32(src[P - LEAD:P, TPI * it - 1, :])).then_inc(s_xrows, 16)
            sp.wait_ge(s_xrows, 16 * (4 + 2 * (2 * ITERS + 2)))
            with sp.Fori(0, ITERS) as I:
                for par in range(2):
                    sp.wait_ge(s_C, AHEAD_C + 16 * I - 8 + 8 * par)
                    for q in range(2):
                        for hl in range(2):
                            for a in range(3):
                                r0 = par * CHUNK + BLK * (q + a)
                                m0, s0 = r0 // (2 * BLK), r0 % (2 * BLK)
                                rows = x_rows[hl].rearrange("i (m s) c -> i m s c", s=2 * BLK)
                                src = rows[I, m0:m0 + CPAIR, s0:s0 + BLK, :].rearrange("m r c -> r m c")
                                row = 64 * q + SEG * a
                                sp.dma_start(f32(xw[par][hl][row:row + BLK, :, :]), src).then_inc(s_win[par], 16)
                            for a in range(2):
                                row = 64 * q + SEG * a + BLK
                                src = bos_rows[hl][I, :].unsqueeze(0).unsqueeze(1).broadcast_to([1, CPAIR, P])
                                sp.dma_start(f32(xw[par][hl][row:row + 1, :, :]), src).then_inc(s_win[par], 16)
            for g in range(ITERS):
                b, h = divmod(g, 2)
                sp.wait_ge(f_out, 4 * g + 4)
                t0, r0 = TPI * g, 1 + ITER_TOK * h
                n = TPI if h == 0 else TPI - 1
                sp.dma_start(out[b, r0:r0 + n * P, :].rearrange("(m p) c -> p m c", p=P),
                             outS[:, t0:t0 + n, :]).then_inc(f_store, 16)
                if h:
                    sp.dma_start(out[b, N - P + 1:N, :], outS[0:P - 1, t0 + 3, :]).then_inc(f_store, 16)
                    sp.dma_start(out[b, 0:1, :], outS[P - 1:P, t0 + 3, :]).then_inc(f_store, 16)
            sp.wait_ge(f_store, 16 * 8)

        @block.gpsimd
        def _(pool):
            nc.gpsimd.memset(ident[:, :], 0.0).then_inc(s_pool, 1)
            pool.wait_ge(s_pool, 1)
            nc.gpsimd.affine_select(out=ident[:, :], in_=ident[:, :], compare_op=ALU.not_equal, fill=1.0,
                                    base=0, pattern=[[-1, P]], channel_multiplier=1).then_inc(s_ident, 1)
            nc.gpsimd.memset(zrow[:, :], 0.0).then_inc(s_zero, 1)
            nc.gpsimd.memset(xT17[:, 0:3:2, 0:2, 0:BLK], 0.0).then_inc(s_zero, 1)
            pool.dma_start(b_sb[:, :], b_out.rearrange("(c o) -> c o", o=1)).then_inc(s_small, 16)
            for k in range(IL):
                pool.dma_start(wth8[k:P:IL, :], w_th).then_inc(s_small, 16)
            for i in range(2):
                nc.gpsimd.memset(E[i][:, :, :], 0.0).then_inc(s_epad, 1)
            for c, value in enumerate(CONSTS):
                nc.gpsimd.memset(consts[:, c, :], value)
            nc.gpsimd.memset(sel[:, :], 0.0).then_inc(s_const, 1)
            m = mask[:, :, :].rearrange("p v (r f q w) -> p v r f q w", r=2, f=2, q=2)
            nc.gpsimd.memset(mask[:, :, :], 0.0).then_inc(s_mask, 1)
            pool.wait_ge(s_mask, 1)
            n = 1
            for v in range(2):
                for r in range(2):
                    for f in range(2):
                        own = m[0:IL, v, r, f, :, 2 * SEG:WIN]
                        nc.gpsimd.affine_select(out=own, in_=own, compare_op=ALU.is_ge, fill=NEG, base=IL * f,
                                                pattern=[[0, 2], [-1, BLK]], channel_multiplier=1).then_inc(s_mask, 1)
                        n += 1
                        nc.gpsimd.memset(m[0:IL, v, r, f, :, 2 * SEG - 1:2 * SEG], NEG)
            for f in range(2):
                nc.gpsimd.memset(m[0:IL, 0, 0, f, :, 0:BLK], NEG)
                nc.gpsimd.memset(m[0:IL, 0, 0, f, 0, SEG:SEG + BLK], NEG).then_inc(s_mask, 1)
            pool.wait_ge(s_asum, 2)
            nc.gpsimd.partition_all_reduce(tsum[:, 2:4], tsum[:, 0:2], P, RADD).then_inc(s_atot, 1)

            with pool.Fori(0, ITERS) as I:
                for j in range(SLOTS):
                    e = E[j % 2][:, :, 0:WIN]
                    pool.wait_ge(s_rec, SLOTS * I + j + 1)
                    nc.gpsimd.tensor_tensor(e, e, rc[j % 2][:, :].unsqueeze(2).broadcast_to([P, TILES, WIN]),
                                            ALU.mult).then_inc(s_norm, 1)

            with pool.Fori(0, ITERS) as g:
                pool.wait_ge(f_var, 4 * g + 4)
                nc.gpsimd.tensor_tensor(vpe[:, :], mv[:, :, 1], consts[:, EPS, :], ALU.add).then_inc(f_eps, 1)
                pool.wait_ge(f_eps, g + 1)
                nc.gpsimd.tensor_tensor(rstd[:, :], vpe[:, :], consts[:, MINUS_HALF, :], ALU.pow).then_inc(f_rstd, 1)
                pool.wait_ge(f_ssq, 4 * g + 4)
                nc.gpsimd.tensor_tensor(rms[:, :], ssq[:, :], consts[:, PER_D, :], ALU.mult).then_inc(f_r1, 1)
                pool.wait_ge(f_r1, g + 1)
                nc.gpsimd.tensor_tensor(rms[:, :], rms[:, :], consts[:, HALF, :], ALU.pow).then_inc(f_rms, 1)
                pool.wait_ge(f_sq, 4 * g + 4)
                nc.gpsimd.tensor_tensor(hrms[:, :], hss[:, :], consts[:, PER_FF, :], ALU.mult).then_inc(f_h1, 1)
                pool.wait_ge(f_h1, g + 1)
                nc.gpsimd.tensor_tensor(hrms[:, :], hrms[:, :], consts[:, HALF, :], ALU.pow).then_inc(f_hrms, 1)
                pool.wait_ge(f_var2, 4 * g + 4)
                nc.gpsimd.tensor_tensor(vpe2[:, :], mv2[:, :, 1], consts[:, EPS, :], ALU.add).then_inc(f_eps2, 1)
                pool.wait_ge(f_eps2, g + 1)
                nc.gpsimd.tensor_tensor(rstd2[:, :], vpe2[:, :], consts[:, MINUS_HALF, :], ALU.pow).then_inc(f_rstd2, 1)

        @block.scalar
        def _(act):
            copy = lambda o, i, **k: nc.scalar.activation(o, i, ACT.Copy, **k)
            for c in range(3):
                act.dma_start(w_sb[:, c * INNER:(c + 1) * INNER], w_qkv[:, c * INNER:(c + 1) * INNER]).then_inc(s_wqkv, 16)
            act.dma_start(w_ff[:, 0, :].rearrange("p (t d) -> p t d", t=FT),
                          w_up.rearrange("(t p) d -> p t d", p=P)).then_inc(s_wff, 16)
            act.dma_start(w_ff[:, 1, :], w_down).then_inc(s_wff, 16)

            def fills(fs):
                for kind, i, bk, who in fs:
                    if "A" not in who:
                        continue
                    act.wait_ge(s_fill, fill_no(kind, i))
                    if kind == "x":
                        copy(xTh[:, 512 * i:512 * (i + 1)], bank[bk][:, :]).then_inc(s_eva, 1)
                    elif kind == "w":
                        copy(wT[:, 4 * i:4 * i + 4, :], bank[bk][:, :].rearrange("p (t c) -> p t c", t=4)).then_inc(s_eva, 1)
                    elif kind == "g":
                        hs = heads(i)
                        copy(Gh[:, hs[0]:hs[-1] + 1:2, :], bank[bk][:, :].rearrange("p (t c) -> p t c", t=4),
                             scale=SCALE).then_inc(s_eva, 1)
                        if i == 1:
                            act.wait_ge(s_xq, 96)
                            copy(xqh[:, :, :], xq[:, :, :]).then_inc(s_xqh, 1)
                    elif kind == "p":
                        hs = heads(i)
                        copy(PT[:, hs[0]:hs[-1] + 1:2, :], bank[bk][:, :].rearrange("p (t c) -> p t c", t=4)).then_inc(s_eva, 1)
                    elif kind == "m":
                        o = Mh[:, :, 32 * i:32 * i + 32].rearrange("p h (a b) -> p a h b", b=IL)
                        copy(o, bank[bk][:, :].rearrange("p (a h b) -> p a h b", a=4, b=IL)).then_inc(s_eva, 1)
                    elif kind == "t":
                        copy(wuT[:, :], bank[bk][:, :]).then_inc(s_eva, 1)

            fills(FILLS)
            act.wait_ge(s_eva, read_no("A", "p", 3))
            act.wait_ge(s_evd, read_no("D", "p", 3))
            act.dma_start(pt_rows, PT[:, :, :]).then_inc(s_pt, 16)
            for b in range(8):
                act.wait_ge(s_Y, b + 1)
                copy(Y_out(b, 0, 2 * b), bank[Y_BANK[b % 2]][:, :].rearrange("p (h t i) -> p h t i", h=2, i=IL)).then_inc(s_Ye, 1)
                if b == 1:
                    act.wait_ge(s_pt, 16)
                    for g in range(H):
                        act.dma_start(R[g * IL:(g + 1) * IL, :, :],
                                      pt_rows.rearrange("(oh ol) g c -> g ol oh c", ol=IL)[g]).then_inc(s_R, 16)
            fills(TAIL)

            def ct_hi(j, t2):
                sc, par = (j - 2) % 4, ((j - 2) // 4) % 2
                for bk in range(2):
                    act.wait_ge(s_C, AHEAD_C + t2 + 1 + bk)
                    copy(ct_view(CTh[par], sc, bk), c_view(bk)).then_inc(s_CTh, 1)

            def at_hi(j, t):
                act.wait_ge(s_T, t)
                copy(ATh[(j - 1) % 2][:, :], bank[T_BANK][:, :]).then_inc(s_ATh, 1)

            act.sem_inc(s_CTh, AHEAD_CT)
            act.sem_inc(s_Oe, AHEAD_OE)
            with act.Fori(0, ITERS) as I:
                for j in range(SLOTS):
                    if j == 2:
                        act.wait_ge(s_O, AHEAD_O + 2 * I - 1)
                    if j == 6:
                        act.wait_ge(s_O, AHEAD_O + 2 * I)
                    with since(act, I, j, 2):
                        ct_hi(j, 16 * I + 2 * j - 4)

                    def y_out(b):
                        with before_last(act, I, j):
                            if j % 4 == 0 and b == 0:
                                act.wait_ge(s_S, SLOTS * I + j)
                            act.wait_ge(s_Y, 16 * I + 2 * j + b + 9)
                            copy(Y_out(b, (j // 4 + 1) % 2, 4 * (j % 4) + 2 * b),
                                 bank[Y_BANK[b]][:, :].rearrange("p (h t i) -> p h t i", h=2, i=IL)).then_inc(s_Ye, 1)
                    y_out(0)
                    e = E[j % 2][:, :, 0:WIN]
                    act.wait_ge(s_sub, AHEAD_SUB + SLOTS * I + j + 1)
                    nc.scalar.activation(e, e, ACT.Exp).then_inc(s_exp, 1)
                    y_out(1)
                    with since(act, I, j, 1):
                        at_hi(j, SLOTS * I + j)
                    if j in (0, 4):
                        with act.If(I > 0):
                            act.wait_ge(s_O, AHEAD_O + 2 * I - 1 + j // 4)
                            copy(attnT[:, bass.ds((2 * I + 2 * ITERS - 2 + j // 4) % (2 * ITERS) * CHUNK, CHUNK)],
                                 bank[O_BANK][:, 0:CHUNK]).then_inc(s_Oe, 1)
            last = SLOTS * ITERS
            ct_hi(0, 2 * last - 4)
            at_hi(0, last)
            act.wait_ge(s_O, AHEAD_O + 2 * ITERS - 1)
            copy(attnT[:, (2 * ITERS - 2) * CHUNK:(2 * ITERS - 1) * CHUNK], bank[O_BANK][:, 0:CHUNK]).then_inc(s_Oe, 1)
            ct_hi(1, 2 * last - 2)
            act.wait_ge(s_O, AHEAD_O + 2 * ITERS)
            copy(attnT[:, (2 * ITERS - 1) * CHUNK:2 * ITERS * CHUNK], bank[O_BANK][:, 0:CHUNK]).then_inc(s_Oe, 1)

            with act.Fori(0, ITERS) as g:
                act.wait_ge(f_xT, g + 1)
                copy(xnTh[:, :], bank[1][:, :]).then_inc(f_xTh, 1)
                for i in range(TPI):
                    act.wait_ge(f_up, 4 * g + i + 1)
                    act.wait_ge(f_hT, 4 * g + max(i - 1, 0))
                    act.wait_ge(f_sq, 4 * g + max(i - 1, 0))
                    nc.scalar.activation(gS[i % 2][:, :], bank[2 + i % 2][:, :], ACT.Gelu).then_inc(f_gelu, 1)

        @block.vector
        def _(dve):
            v = nc.vector
            dve.wait_ge(s_ident, 1)
            v.tensor_reduce(sel8[:, :], ident[:, :].rearrange("p (g k) -> p k g", k=IL), AX.X, ALU.add).then_inc(s_sel8, 1)
            dve.wait_ge(s_const, 1)
            v.tensor_copy(sel[0:IL, :].rearrange("p (h k) -> p h k", k=IL),
                          ident[0:IL, 0:IL].unsqueeze(1).broadcast_to([IL, H, IL])).then_inc(s_sel, 1)

            def fills(fs):
                for kind, i, bk, who in fs:
                    if "D" not in who:
                        continue
                    dve.wait_ge(s_fill, fill_no(kind, i))
                    if kind == "x":
                        dve.wait_ge(s_eva, read_no("A", kind, i))
                        v.tensor_copy(xT17[:, i, 2:IBLK + 2, 0:BLK], bank[bk][:, :].rearrange("p (u s) -> p u s", s=BLK))
                        if i % 2 == 0:
                            v.tensor_copy(xT17[:, i + 1, 0:2, 0:BLK],
                                          bank[bk][:, 512 - LEAD:512].rearrange("p (u s) -> p u s", s=BLK))
                        else:
                            v.tensor_copy(xT17[:, i - 1:i + 1, :, BLK],
                                          bank[bk][:, 511:512].unsqueeze(2).broadcast_to([P, 2, IBLK + 2]))
                        o = slice(512 * i, 512 * (i + 1))
                        v.tensor_tensor(xTl[:, o], bank[bk][:, :], f32(xTh[:, o]), ALU.subtract).then_inc(s_evd, 1)
                    elif kind == "w":
                        v.tensor_copy(wT[:, 4 * i:4 * i + 4, :], bank[bk][:, :].rearrange("p (t c) -> p t c", t=4)).then_inc(s_evd, 1)
                    elif kind == "g":
                        hs = heads(i)
                        o = slice(hs[0], hs[-1] + 1, 2)
                        dve.wait_ge(s_eva, read_no("A", kind, i))
                        v.scalar_tensor_tensor(out=Gl[:, o, :], in0=bank[bk][:, :].rearrange("p (t c) -> p t c", t=4),
                                               scalar=SCALE, in1=f32(Gh[:, o, :]), op0=ALU.mult,
                                               op1=ALU.subtract).then_inc(s_evd, 1)
                    elif kind == "p":
                        hs = heads(i)
                        v.tensor_copy(PT[:, hs[0]:hs[-1] + 1:2, :], bank[bk][:, :].rearrange("p (t c) -> p t c", t=4)).then_inc(s_evd, 1)
                    elif kind == "m":
                        o = slice(32 * i, 32 * i + 32)
                        dve.wait_ge(s_eva, read_no("A", kind, i))
                        v.tensor_tensor(Ml[:, :, o].rearrange("p h (a b) -> p a h b", b=IL),
                                        bank[bk][:, :].rearrange("p (a h b) -> p a h b", a=4, b=IL),
                                        f32(Mh[:, :, o]).rearrange("p h (a b) -> p a h b", b=IL),
                                        ALU.subtract).then_inc(s_evd, 1)
                    elif kind == "t":
                        v.tensor_copy(wdT[:, :, :], bank[bk][:, :].rearrange("p (t c) -> p t c", t=4)).then_inc(s_evd, 1)
                    elif kind == "v0":
                        v.tensor_copy(v0T[:, :], bank[bk][:, 0:16]).then_inc(s_evd, 1)
                    elif kind == "bos":
                        v.tensor_copy(bosT[:, :], bank[bk][:, 0:B]).then_inc(s_evd, 1)

            fills(FILLS)
            dve.wait_ge(s_xqh, 1)
            v.tensor_tensor(xql[:, :, :], xq[:, :, :], f32(xqh[:, :, :]), ALU.subtract).then_inc(s_xql, 1)
            dve.wait_ge(s_small, 16 * (IL + 1))
            dve.wait_ge(s_sel8, 1)
            v.tensor_tensor(kron[:, :].rearrange("p (h k) -> p h k", k=IL),
                            wth8[:, :].unsqueeze(2).broadcast_to([P, H, IL]),
                            sel8[:, :].unsqueeze(1).broadcast_to([P, H, IL]), ALU.mult).then_inc(s_kron, 1)
            dve.wait_ge(s_wff, 32)
            for k in range(2):
                v.tensor_reduce(tsum[:, k:k + 1], w_ff[:, k, :], AX.X, ALU.add, apply_absolute_value=True).then_inc(s_asum, 1)
            dve.wait_ge(s_atot, 1)
            v.tensor_scalar(tsum[:, 4:6], tsum[:, 2:4], 1.0 / (FF * D), 0.5, ALU.mult, ALU.mult).then_inc(s_thr, 1)
            v.tensor_scalar(tsum[:, 6:8], tsum[:, 2:4], 1.0 / (FF * D), -0.5, ALU.mult, ALU.mult).then_inc(s_thr, 1)
            dve.wait_ge(s_thr, 2)
            for k in range(2):
                v.tensor_scalar(tern[:, k, :], w_ff[:, k, :], tsum[:, 6 + k:7 + k], None, ALU.is_lt).then_inc(s_ternd, 1)
            dve.wait_ge(s_ternd, 2)
            for k in range(2):
                v.scalar_tensor_tensor(out=w_ff[:, k, :], in0=w_ff[:, k, :], scalar=tsum[:, 4 + k:5 + k],
                                       in1=tern[:, k, :], op0=ALU.is_gt, op1=ALU.subtract).then_inc(s_tern, 1)
            fills(TAIL)

            def ct_lo(j, t2):
                sc, par = (j - 2) % 4, ((j - 2) // 4) % 2
                for bk in range(2):
                    dve.wait_ge(s_CTh, AHEAD_CT + t2 + 1 + bk)
                    v.tensor_tensor(ct_view(CTl[par], sc, bk), c_view(bk), ct_view(f32(CTh[par][:, :, :]), sc, bk),
                                    ALU.subtract).then_inc(s_CTl, 1)

            def at_lo(j, t):
                dve.wait_ge(s_ATh, t)
                v.tensor_tensor(ATl[(j - 1) % 2][:, :], bank[T_BANK][:, :], f32(ATh[(j - 1) % 2][:, :]),
                                ALU.subtract).then_inc(s_ATl, 1)

            dve.sem_inc(s_CTl, AHEAD_CT)
            dve.sem_inc(s_sub, AHEAD_SUB)
            dve.sem_inc(s_ATl, AHEAD_ATL)
            with dve.Fori(0, ITERS) as I:
                for j in range(SLOTS):
                    k = j % 2
                    with since(dve, I, j, 2):
                        ct_lo(j, 16 * I + 2 * j - 4)
                    s = bank[S_BANK[k]][:, 0:TILES * WIN].rearrange("p (t w) -> p t w", w=WIN)
                    e = E[k][:, :, 0:WIN]
                    dve.wait_ge(s_S, SLOTS * I + j + 1)
                    v.tensor_reduce(mx[k][:, :], s, AX.X, ALU.max).then_inc(s_max, 1)
                    dve.wait_ge(s_max, SLOTS * I + j + 1)
                    v.tensor_tensor(e, s, mx[k][:, :].unsqueeze(2).broadcast_to([P, TILES, WIN]),
                                    ALU.subtract).then_inc(s_sub, 1)
                    dve.wait_ge(s_exp, SLOTS * I + j + 1)
                    v.tensor_reduce(sm[k][:, :], e, AX.X, ALU.add).then_inc(s_sum, 1)
                    dve.wait_ge(s_sum, SLOTS * I + j + 1)
                    v.reciprocal(rc[k][:, :], sm[k][:, :]).then_inc(s_rec, 1)
                    with since(dve, I, j, 1):
                        at_lo(j, SLOTS * I + j)
            last = SLOTS * ITERS
            ct_lo(0, 2 * last - 4)
            at_lo(0, last)
            ct_lo(1, 2 * last - 2)

            dve.wait_ge(s_Oe, AHEAD_OE + 2 * ITERS)
            for b in range(B):
                v.tensor_copy(attnT[:, b * N + N - 1:b * N + N], bosT[:, b:b + 1]).then_inc(f_bosput, 1)
            dve.wait_ge(f_bosput, B)

            with dve.Fori(0, ITERS) as g:
                dve.wait_ge(f_aT, g)
                v.tensor_scalar(attnS[:, :], attnT[:, bass.ds(g * ITER_TOK, ITER_TOK)], b_sb[:, 0:1], None,
                                ALU.add).then_inc(f_stage, 1)
                dve.wait_ge(f_aT, g + 1)
                v.tensor_tensor(res[:, :, :], bank[0][:, :].rearrange("p (t c) -> p t c", t=TPI),
                                xq[:, bass.ds(g * TPI, TPI), :], ALU.add).then_inc(f_res, 1)
                dve.wait_ge(f_res, g + 1)
                for i in range(TPI):
                    v.bn_stats(st[:, i, :], res[:, i, :]).then_inc(f_st, 1)
                dve.wait_ge(f_st, 4 * g + 4)
                dve.sem_inc(f_seen, 1)
                for i in range(TPI):
                    v.bn_aggr(mv[:, i, :], st[:, i, :]).then_inc(f_var, 1)
                dve.wait_ge(f_rstd, g + 1)
                for i in range(TPI):
                    v.tensor_scalar(x1[:, i, :], res[:, i, :], mv[:, i, 0:1], rstd[:, i:i + 1], ALU.subtract,
                                    ALU.mult).then_inc(f_x1, 1)
                for i in range(TPI):
                    dve.wait_ge(f_x1, 4 * g + i + 1)
                    v.tensor_tensor_reduce(out=xn[:, i, :], in0=x1[:, i, :], in1=x1[:, i, :], scale=1.0, scalar=0.0,
                                           op0=ALU.mult, op1=ALU.add, accum_out=ssq[:, i:i + 1]).then_inc(f_ssq, 1)
                dve.wait_ge(f_rms, g + 1)
                v.tensor_scalar(inv[:, :], rms[:, :], EPS_RMS, None, ALU.add).then_inc(f_inv, 1)
                dve.wait_ge(f_inv, 2 * g + 1)
                v.reciprocal(inv[:, :], inv[:, :]).then_inc(f_inv, 1)
                dve.wait_ge(f_inv, 2 * g + 2)
                for i in range(TPI):
                    v.tensor_scalar(xn[:, i, :], x1[:, i, :], inv[:, i:i + 1], None, ALU.mult).then_inc(f_xn, 1)
                dve.wait_ge(f_xTh, g + 1)
                v.tensor_tensor(xnTl[:, :], bank[1][:, :], f32(xnTh[:, :]), ALU.subtract).then_inc(f_xTl, 1)
                for i in range(TPI):
                    dve.wait_ge(f_sq, 4 * g + i)
                    dve.wait_ge(f_gelu, 4 * g + i + 1)
                    v.tensor_tensor_reduce(out=sq[:, :], in0=gS[i % 2][:, :], in1=gS[i % 2][:, :], scale=1.0, scalar=0.0,
                                           op0=ALU.mult, op1=ALU.add, accum_out=hss[:, i:i + 1]).then_inc(f_sq, 1)
                    dve.wait_ge(f_hT, 4 * g + i + 1)
                    dve.wait_ge(f_dn, 4 * g + max(i - 1, 0))
                    v.tensor_copy(hT[i % 2][:, :, :],
                                  bank[4 + i % 2][:, :].rearrange("p (t c) -> p t c", t=FT)).then_inc(f_hTe, 1)
                    if i == TPI - 1:
                        dve.wait_ge(f_hrms, g + 1)
                        v.tensor_scalar(hinv[:, :], hrms[:, :], EPS_RMS, None, ALU.add).then_inc(f_hinv, 1)
                        dve.wait_ge(f_hinv, 2 * g + 1)
                        v.reciprocal(hinv[:, :], hinv[:, :]).then_inc(f_hinv, 1)
                        dve.wait_ge(f_hinv, 2 * g + 2)
                dve.wait_ge(f_dn, 4 * g + 4)
                for i in range(TPI):
                    v.scalar_tensor_tensor(out=y2[:, i, :], in0=bank[6 + i // 2][:, (i % 2) * P:(i % 2) * P + P],
                                           scalar=hinv[:, i:i + 1], in1=x1[:, i, :], op0=ALU.mult,
                                           op1=ALU.add).then_inc(f_y2, 1)
                for i in range(TPI):
                    dve.wait_ge(f_y2, 4 * g + i + 1)
                    v.bn_stats(st2[:, i, :], y2[:, i, :]).then_inc(f_st2, 1)
                dve.wait_ge(f_st2, 4 * g + 4)
                dve.sem_inc(f_seen, 1)
                for i in range(TPI):
                    v.bn_aggr(mv2[:, i, :], st2[:, i, :]).then_inc(f_var2, 1)
                dve.wait_ge(f_rstd2, g + 1)
                for i in range(TPI):
                    v.tensor_scalar(outS[:, bass.ds(g * TPI + i, 1), :], y2[:, i:i + 1, :], mv2[:, i, 0:1], rstd2[:, i:i + 1],
                                    ALU.subtract, ALU.mult).then_inc(f_out, 1)

        @block.tensor
        def _(pe):
            mm = nc.tensor.matmul

            def split3(o, wh, wl, rh, rl, start=True, stop=True, **k):
                mm(o, wh, rh, start=start, stop=False, **k)
                mm(o, wh, rl, start=False, stop=False, **k)
                return mm(o, wl, rh, start=False, stop=stop, **k)

            def y_part(bk, chunk_cols, h0):
                for n in range(2):
                    ins = split3(bank[Y_BANK[bk]][:, CHUNK * n:CHUNK * (n + 1)], Gh[:, h0 + n, :], Gl[:, h0 + n, :],
                                 xTh[:, chunk_cols], xTl[:, chunk_cols])
                ins.then_inc(s_Y, 1)

            def fills(fs):
                for kind, i, bk, who in fs:
                    bank_free(pe, kind, i)
                    bnk = bank[bk]
                    if kind == "x":
                        if i == 0:
                            pe.wait_ge(s_ident, 1)
                            pe.wait_ge(s_xq, 96)
                        for k in range(4):
                            ins = nc.tensor.transpose(bnk[:, P * k:P * k + P], xq[:, 4 * i + k, :], ident[:, :])
                    elif kind == "w":
                        pe.wait_ge(s_wqkv, 48)
                        for k in range(4):
                            c = P * (4 * i + k)
                            ins = nc.tensor.transpose(bnk[:, P * k:P * k + P], w_sb[:, c:c + P], ident[:, :])
                    elif kind == "g":
                        if i == 0:
                            for n in range(4):
                                pe.wait_ge(s_eva if n % 2 == 0 else s_evd, read_no("AD"[n % 2], "w", n))
                        for k, h in enumerate(heads(i)):
                            r = slice(DH * (h % 2), DH * (h % 2) + DH)
                            ins = mm(bnk[:, P * k:P * k + P], wT[r, h // 2, :], wT[r, 8 + h // 2, :], start=True, stop=True)
                    elif kind == "p":
                        if i == 0:
                            pe.wait_ge(s_wout, 16)
                            for n in (4, 5):
                                pe.wait_ge(s_eva if n % 2 == 0 else s_evd, read_no("AD"[n % 2], "w", n))
                        for k, h in enumerate(heads(i)):
                            r = slice(DH * (h % 2), DH * (h % 2) + DH)
                            ins = mm(bnk[:, P * k:P * k + P], wo_sb[r, h // 2, :], wT[r, 16 + h // 2, :], start=True, stop=True)
                    elif kind == "m":
                        if i == 0:
                            pe.wait_ge(s_R, 16 * H)
                            pe.wait_ge(s_kron, 1)
                        for k in range(4):
                            ins = mm(bnk[:, P * k:P * k + P], R[:, 4 * i + k, :], kron[:, :], start=True, stop=True)
                    elif kind == "t":
                        pe.wait_ge(s_tern, 2)
                        for k in range(4):
                            ins = nc.tensor.transpose(bnk[:, P * k:P * k + P], w_ff[:, i, P * k:P * k + P], ident[:, :])
                    elif kind == "v0":
                        for k in range(8):
                            c = 2 * INNER + P * k
                            ins = mm(bnk[:, 2 * k:2 * k + 2], w_sb[:, c:c + P], xT17[:, 0:3:2, 0, BLK], start=True, stop=True)
                    elif kind == "bos":
                        pe.wait_ge(s_evd, read_no("D", "v0", 0))
                        for k in range(8):
                            ins = mm(bnk[:, 0:2], wo_sb[:, k, :], v0T[:, 2 * k:2 * k + 2], start=(k == 0), stop=(k == 7))
                    ins.then_inc(s_fill, 1)

            fills(FILLS)
            pe.wait_ge(s_eva, read_no("A", "g", 3))
            pe.wait_ge(s_evd, read_no("D", "g", 3))
            for b in range(8):
                if b >= 2:
                    pe.wait_ge(s_Ye, b - 1)
                y_part(b % 2, slice(0, CHUNK), 2 * b)
            fills(TAIL)
            pe.wait_ge(s_eva, read_no("A", "bos", 0))
            pe.wait_ge(s_evd, read_no("D", "bos", 0))
            pe.wait_ge(s_zero, 2)
            pe.wait_ge(s_mask, MASKS)
            pe.wait_ge(s_sel, 1)

            def transposes(j, t):
                pe.wait_ge(s_norm, t)
                for r in range(2):
                    for f in range(2):
                        o = bank[T_BANK][:, 256 * r:256 * r + 256].rearrange("p (h s) -> p h s", s=BLK)
                        k = 4 * r + 2 * f
                        ins = nc.tensor.transpose(o[:, :, IL * f:IL * f + IL],
                                                  E[(j - 1) % 2][:, k:k + 2, :].rearrange("p t w -> p (t w)"), ident[:, :])
                ins.then_inc(s_T, 1)

            def c_part(j):
                sc, par, k = (j - 1) % 4, ((j - 1) // 4) % 2, (j - 1) % 2
                for r in range(2):
                    ins = []
                    for q in range(2):
                        row, col = slice(64 * q, 64 * q + WIN), slice(256 * r, 256 * r + 256)
                        m = 2 * sc + r
                        ins.append(split3(bank[C_BANK[q]][:, col], xw[par][0][row, m, :], xw[par][1][row, m, :],
                                          ATh[k][row, col], ATl[k][row, col]))
                for i in ins:
                    i.then_inc(s_C, 1)

            def o_part(p, par):
                for h in range(4 * p, 4 * p + 4):
                    ins = split3(bank[O_BANK][:, 0:CHUNK], Mh[:, h, :], Ml[:, h, :], CTh[par][:, h, :], CTl[par][:, h, :],
                                 start=(h == 0), stop=(h == H - 1))
                if p == 3:
                    ins.then_inc(s_O, 1)

            pe.sem_inc(s_C, AHEAD_C)
            pe.sem_inc(s_O, AHEAD_O)
            with pe.Fori(0, ITERS) as I:
                for j in range(SLOTS):
                    k = j % 2
                    pe.wait_ge(s_sub, AHEAD_SUB + SLOTS * I + j - 1)
                    if j % 4 == 0:
                        pe.wait_ge(s_Ye, 16 * I + 2 * j + 8)
                    v = bass.ds(I % 2, 1) if j == 0 else slice(1, 2)
                    mm(bank[S_BANK[k]][:, 0:TILES * WIN], sel[:, :], mask[:, v, :].rearrange("p a w -> p (a w)"),
                       start=True, stop=False)
                    for tile in range(TILES):
                        r, f, q = tile // 4, tile // 2 % 2, tile % 2
                        blk = STEP_BLK * j + 2 * r + q
                        ytile = 2 * (blk % CBLK) + f
                        keys = xT17[:, bass.ds(I, 1), :, :].rearrange("p i u s -> p (i u s)")[:, SEG * blk:SEG * blk + WIN]
                        ins = mm(bank[S_BANK[k]][:, WIN * tile:WIN * tile + WIN], Yb[(j // 4) % 2][:, ytile, :], keys,
                                 start=False, stop=(tile == TILES - 1))
                    ins.then_inc(s_S, 1)
                    with before_last(pe, I, j):
                        for b in range(2):
                            pe.wait_ge(s_Ye, 16 * I + 2 * j + b + 7)
                            y_part(b, bass.ds((2 * I + j // 4 + 1) % (2 * ITERS) * CHUNK, CHUNK), 4 * (j % 4) + 2 * b)
                    with since(pe, I, j, 1):
                        pe.wait_ge(s_ATl, AHEAD_ATL + SLOTS * I + j - 1)
                        transposes(j, SLOTS * I + j)
                    with since(pe, I, j, 5):
                        n, p = divmod(j + 3, 4)
                        if p == 0:
                            pe.wait_ge(s_CTl, AHEAD_CT + 8 * (2 * I + n - 1))
                            pe.wait_ge(s_Oe, AHEAD_OE + 2 * I + n - 2)
                        o_part(p, n % 2)
                    with since(pe, I, j, 1):
                        pe.wait_ge(s_ATl, AHEAD_ATL + SLOTS * I + j)
                        pe.wait_ge(s_CTl, AHEAD_CT + 16 * I + 2 * j - 2)
                        if j in (1, 5):
                            pe.wait_ge(s_win[j // 4], 16 * WDMAS * (I + 1))
                        c_part(j)
            last = SLOTS * ITERS
            pe.wait_ge(s_ATl, AHEAD_ATL + last - 1)
            transposes(0, last)
            o_part(3, 0)
            pe.wait_ge(s_ATl, AHEAD_ATL + last)
            pe.wait_ge(s_CTl, AHEAD_CT + 2 * last - 2)
            c_part(0)
            pe.wait_ge(s_CTl, AHEAD_CT + 2 * last)
            pe.wait_ge(s_Oe, AHEAD_OE + 2 * ITERS - 1)
            for p in range(4):
                o_part(p, 1)

            with pe.Fori(0, ITERS) as g:
                pe.wait_ge(f_res, g)
                pe.wait_ge(f_stage, g + 1)
                for i in range(TPI):
                    ins = nc.tensor.transpose(bank[0][:, P * i:P * i + P], attnS[:, P * i:P * i + P], ident[:, :])
                ins.then_inc(f_aT, 1)
                pe.wait_ge(f_xTl, g)
                pe.wait_ge(f_xn, 4 * g + 4)
                for i in range(TPI):
                    ins = nc.tensor.transpose(bank[1][:, P * i:P * i + P], xn[:, i, :], ident[:, :])
                ins.then_inc(f_xT, 1)
                pe.wait_ge(f_xTl, g + 1)
                for i in range(TPI + 2):
                    if i < TPI:
                        c = slice(P * i, P * i + P)
                        mm(bank[2 + i % 2][:, :], xnTh[:, c], wuT[:, :], start=True, stop=False)
                        mm(bank[2 + i % 2][:, :], xnTl[:, c], wuT[:, :], start=False, stop=True).then_inc(f_up, 1)
                    if 1 <= i <= TPI:
                        pe.wait_ge(f_gelu, 4 * g + i)
                        for k in range(FT):
                            ins = nc.tensor.transpose(bank[4 + (i - 1) % 2][:, P * k:P * k + P],
                                                      gS[(i - 1) % 2][:, P * k:P * k + P], ident[:, :])
                        ins.then_inc(f_hT, 1)
                    if i >= 2:
                        n = i - 2
                        pe.wait_ge(f_hTe, 4 * g + n + 1)
                        if n == 0:
                            pe.wait_ge(f_y2, 4 * g)
                        for k in range(FT):
                            ins = mm(bank[6 + n // 2][:, (n % 2) * P:(n % 2) * P + P], hT[n % 2][:, k, :], wdT[:, k, :],
                                     start=(k == 0), stop=(k == FT - 1))
                        ins.then_inc(f_dn, 1)


_INS = ["L0_attn_x", "L0_attn_w_qkv", "L0_attn_w_out", "L0_attn_b_out", "L0_attn_w_th", "L0_ffn_w_up", "L0_ffn_w_down"]


def kernel(**inputs):
    import numpy as np
    import concourse.bacc as bacc
    from concourse.bass_utils import run_bass_kernel_spmd

    nc = bacc.Bacc("TRN2", target_bir_lowering=False, num_devices=1)
    arrays, args = {}, []
    for name in _INS:
        a = np.ascontiguousarray(inputs[name])
        arrays[f"in_{name}"] = a
        args.append(nc.dram_tensor(f"in_{name}", a.shape, mybir.dt.from_np(a.dtype), kind="ExternalInput").ap())
    out = nc.dram_tensor("out", (B, N, D), F32, kind="ExternalOutput").ap()
    x_rows = [nc.dram_tensor(f"x_rows{s}", (ITERS, XROWS, D), F32, kind="Internal").ap() for s in "hl"]
    bos_rows = [nc.dram_tensor(f"bos_rows{s}", (ITERS, D), F32, kind="Internal").ap() for s in "hl"]
    pt_rows = nc.dram_tensor("pt_rows", (P, H, P), F32, kind="Internal").ap()
    attention_ffn(nc, *args, out, x_rows, bos_rows, pt_rows)
    r = run_bass_kernel_spmd(nc, [arrays], core_ids=[0])
    return r.results[0]["out"]
```

```python
import concourse.bass as bass
from concourse import mybir
from contextlib import ExitStack, nullcontext

F32 = mybir.dt.float32
F32R = mybir.dt.float32r
BF16 = mybir.dt.bfloat16
ALU = mybir.AluOpType
ACT = mybir.ActivationFunctionType
AX = mybir.AxisListType
RADD = bass.bass_isa.ReduceOp.add

B, N, D = 2, 1024, 128
H, DH = 16, 64
INNER = H * DH
FF = 512
P = 128
BLK = 16
SEG = BLK + 1
WIN = 3 * SEG - 1
PITCH = 64
IL = 8
ITER_TOK = 512
ITERS = B * N // ITER_TOK
IBLK = ITER_TOK // BLK
CHUNK = 256
CBLK = CHUNK // BLK
CPAIR = CBLK // 2
STEP_BLK = 4
SLOTS = IBLK // STEP_BLK
TILES = 2 * STEP_BLK
NEG = -float(2.0 ** 100)
XCOLS = (IBLK + 2) * SEG
LEAD = 2 * BLK
XROWS = LEAD + ITER_TOK
SCALE = float(DH) ** -0.5
EPS_LN, EPS_RMS = 1e-5, 1e-8
TPI = ITER_TOK // P
NT = B * N // P
FT = FF // P
CONSTS = (-0.5, 0.5, -1.0, EPS_LN, EPS_RMS, 1.0 / FF)
MINUS_HALF, HALF, MINUS_ONE, C_EPS_LN, C_EPS_RMS, C_PER_FF = range(6)


def attention_ffn(nc, x, w_qkv, w_out, b_out, w_th, w_up, w_down, out, x_rows, bos_rows, pt_rows):
    ctx = ExitStack()
    with ctx:
        def sb(name, shape, dt=F32):
            return ctx.enter_context(nc.sbuf_tensor(name, shape, dt))

        def sem(name):
            return ctx.enter_context(nc.semaphore(name))

        ident = sb("ident", [P, P])
        sel = sb("sel", [P, P], BF16)
        mask = sb("mask", [P, 2, TILES * WIN], BF16)
        sel8 = sb("sel8", [P, IL])
        wth8 = sb("wth8", [P, H])
        kron = sb("kron", [P, P])
        zrow = sb("zrow", [LEAD, 2 * P])
        tsum = sb("tsum", [P, 8])
        v0T = sb("v0T", [P, 8 * B])
        consts = sb("consts", [P, len(CONSTS), TPI])
        b_sb = sb("b_sb", [P, 1])
        Gh = sb("Gh", [P, H, P], F32R)
        Gl = sb("Gl", [P, H, P], F32R)
        Mh = sb("Mh", [P, H, P], F32R)
        Ml = sb("Ml", [P, H, P], F32R)
        bosT = sb("bosT", [P, B])
        wuT = sb("wuT", [P, FF], F32R)
        wdT = sb("wdT", [P, FT, P], F32R)
        xq = sb("xq", [P, NT, P])
        xTh = sb("xTh", [P, B * N], F32R)
        xTl = sb("xTl", [P, B * N], F32R)
        xT17 = sb("xT17", [P, ITERS, IBLK + 2, SEG])
        xw = [sb(f"xw{i}", [P, CPAIR, 2, P], F32R) for i in range(2)]
        attnT = sb("attnT", [P, B * N])

        with ExitStack() as prep:
            def pb(name, shape, dt=F32):
                return prep.enter_context(nc.sbuf_tensor(name, shape, dt))

            w_sb = pb("w_sb", [P, 3 * INNER])
            wT = pb("wT", [P, 24, P])
            wo_sb = pb("wo_sb", [P, 8, P])
            wo_p = pb("wo_p", [P, 8, IL, H])
            PT = pb("PT", [P, H, P])
            R = pb("R", [P, H, P])
            xs = pb("xs", [P, NT, 2, P])
            w_ff = pb("w_ff", [P, 2, FF])
            tern = pb("tern", [P, 2, FF])
        with ExitStack() as attention:
            def ab(name, shape, dt=F32):
                return attention.enter_context(nc.sbuf_tensor(name, shape, dt))

            CTh = [ab(f"CTh{i}", [P, H, CHUNK], F32R) for i in range(2)]
            CTl = [ab(f"CTl{i}", [P, H, CHUNK], F32R) for i in range(2)]
            ATh = [ab(f"ATh{i}", [P, 512], F32R) for i in range(2)]
            ATl = [ab(f"ATl{i}", [P, 512], F32R) for i in range(2)]
            Yb = [ab(f"Yb{i}", [P, CHUNK // IL, P]) for i in range(2)]
            E = [ab(f"E{i}", [P, TILES, PITCH]) for i in range(2)]
            mx = [ab(f"mx{i}", [P, TILES]) for i in range(2)]
            sm = [ab(f"sm{i}", [P, TILES]) for i in range(2)]
            rc = [ab(f"rc{i}", [P, TILES]) for i in range(2)]
        attnS = sb("attnS", [P, ITER_TOK])
        res = sb("res", [P, TPI, P])
        x1 = sb("x1", [P, TPI, P])
        x1all = sb("x1all", [P, NT, P])
        x1Th = sb("x1Th", [P, ITER_TOK], F32R)
        x1Tl = sb("x1Tl", [P, ITER_TOK], F32R)
        gS = [sb(f"gS{i}", [P, FF]) for i in range(2)]
        sq = sb("sq", [P, FF])
        hTh = sb("hTh", [P, FT, ITER_TOK], F32R)
        hTl = sb("hTl", [P, FT, ITER_TOK], F32R)
        dS = sb("dS", [P, ITER_TOK])
        y2 = sb("y2", [P, TPI, P])
        outS = sb("outS", [P, TPI, P])
        st = sb("st", [P, TPI, 6])
        mv = sb("mv", [P, TPI, 2])
        st2 = sb("st2", [P, TPI, 6])
        mv2 = sb("mv2", [P, TPI, 2])
        inv = sb("inv", [P, NT])
        hss = sb("hss", [P, TPI])
        hinv = sb("hinv", [P, TPI])
        rstd = sb("rstd", [P, TPI])
        rstd2 = sb("rstd2", [P, TPI])
        tiny = sb("tiny", [P, 8, TPI])

        bank = [ctx.enter_context(nc.psum_tensor(f"bank{i}", [P, 512], F32)) for i in range(8)]
        S_BANK, Y_BANK, T_BANK, C_BANK, O_BANK = [0, 1], [2, 3], 4, [5, 6], 7

        s_xq = [sem(f"s_xq{b}") for b in range(B)]
        s_wqkv = [sem(f"s_wqkv{c}") for c in range(3)]
        s_wout, s_small, s_wff = map(sem, ("s_wout", "s_small", "s_wff"))
        s_ident, s_pool, s_const, s_sel8, s_kron, s_zero, s_epad = map(sem, (
            "s_ident", "s_pool", "s_const", "s_sel8", "s_kron", "s_zero", "s_epad"))
        s_fill, s_eva, s_evd = map(sem, ("s_fill", "s_evac_act", "s_evac_dve"))
        s_wop, s_xsh, s_xsl, s_xrows, s_pt, s_R = map(sem, ("s_wop", "s_xsh", "s_xsl", "s_xrows", "s_pt", "s_R"))
        s_asum, s_atot, s_thr, s_ternd, s_tern = map(sem, ("s_asum", "s_atot", "s_thr", "s_ternd", "s_tern"))
        s_mask, s_sel = sem("s_mask"), sem("s_sel")
        MASKS = 1 + 2 * 4 + 2
        s_win = [sem("s_win0"), sem("s_win1")]
        s_Y, s_Ye = sem("s_Y"), sem("s_Ye")
        s_S, s_max, s_sub, s_exp, s_sum, s_rec, s_norm = map(sem, (
            "s_S", "s_max", "s_sub", "s_exp", "s_sum", "s_rec", "s_norm"))
        s_T, s_ATh, s_ATl = map(sem, ("s_T", "s_ATh", "s_ATl"))
        s_C, s_CTh, s_CTl = map(sem, ("s_C", "s_CTh", "s_CTl"))
        s_O, s_Oe = sem("s_O"), sem("s_Oe")
        f_stage, f_aT, f_res, f_st, f_var, f_eps, f_rstd, f_x1, f_x1c, f_xT, f_xTh, f_xTl = map(sem, (
            "f_stage", "f_aT", "f_res", "f_st", "f_var", "f_eps", "f_rstd", "f_x1", "f_x1c", "f_xT", "f_xTh", "f_xTl"))
        f_rms, f_inv, f_hrms, f_hinv, f_eps2, f_rstd2 = map(sem, (
            "f_rms", "f_inv", "f_hrms", "f_hinv", "f_eps2", "f_rstd2"))
        f_up, f_gelu, f_sq, f_hT, f_hTh, f_hTl, f_dn, f_dnE, f_back = map(sem, (
            "f_up", "f_gelu", "f_sq", "f_hT", "f_hTh", "f_hTl", "f_dn", "f_dnE", "f_back"))
        f_y2, f_st2, f_var2, f_out, f_store, f_bosput, f_seen = map(sem, (
            "f_y2", "f_st2", "f_var2", "f_out", "f_store", "f_bosput", "f_seen"))
        f_seen_pool, f_seen_act = sem("f_seen_pool"), sem("f_seen_act")

        FILLS = ([("x", i, i, "AD") for i in range(4)]
                 + [("w", i, (4, 5, 6, 7, 0, 1)[i], "A" if i % 2 == 0 else "D") for i in range(4)]
                 + [("g", i, i, "AD") for i in range(4)]
                 + [("w", i, (4, 5)[i - 4], "A" if i % 2 == 0 else "D") for i in (4, 5)]
                 + [("p", i, (6, 7, 0, 1)[i], "A" if i % 2 == 0 else "D") for i in range(4)])
        TAIL = ([("m", i, (4, 5, 6, 7)[i], "AD") for i in range(4)]
                + [("t", 0, 0, "A"), ("t", 1, 1, "D"), ("v0", 0, 4, "D"), ("bos", 0, 5, "D")])
        ALLF = FILLS + TAIL

        def fill_no(kind, i):
            return next(n for n, f in enumerate(ALLF) if f[:2] == (kind, i)) + 1

        def read_no(who, kind, i):
            return sum(who in f[3] for f in ALLF[:fill_no(kind, i)])

        def bank_free(eng, kind, i):
            n = fill_no(kind, i) - 1
            for before in reversed(ALLF[:n]):
                if before[2] == ALLF[n][2]:
                    if "A" in before[3]:
                        eng.wait_ge(s_eva, read_no("A", *before[:2]))
                    if "D" in before[3]:
                        eng.wait_ge(s_evd, read_no("D", *before[:2]))
                    return

        WDMAS = 2 * (3 + 1)

        AHEAD_SUB = AHEAD_ATL = AHEAD_O = AHEAD_OE = 1
        AHEAD_C, AHEAD_CT = 8, 4
        AHEAD_GELU = AHEAD_HT = AHEAD_HTL = AHEAD_SQ = 1
        AHEAD_OUT = AHEAD_Y2 = TPI
        AHEAD_HRMS = 3
        AHEAD_STORE = 16 * (TPI + 1)

        def since(eng, I, j, d):
            return nullcontext() if j >= d else eng.If(I > 0)

        def before_last(eng, I, j):
            return nullcontext() if j < SLOTS // 2 else eng.If(I < ITERS - 1)

        def heads(i):
            return [8 * (i // 2) + i % 2 + 2 * k for k in range(4)]

        def Y_out(b, chunk_par, h0):
            return Yb[chunk_par][:, :, IL * h0:IL * h0 + 2 * IL].rearrange("p t (h i) -> p h t i", i=IL)

        def ct_view(buf, sc, q):
            v = buf[:, :, :].rearrange("p h (r q s) -> p h r q s", q=2, s=BLK)
            return v[:, :, 2 * sc:2 * sc + 2, q, :].rearrange("p h r s -> p r h s")

        def c_view(bk):
            return bank[C_BANK[bk]][:, :].rearrange("p (r h s) -> p r h s", r=2, s=BLK)

        def f32(ap):
            return ap.bitcast(F32)

        block = ctx.enter_context(nc.Block())

        @block.sync
        def _(sp):
            for b in range(B):
                t0 = b * (NT // B)
                sp.dma_start(xq[:, t0:t0 + 7, :], x[b, 1:897, :].rearrange("(m p) c -> p m c", p=P)).then_inc(s_xq[b], 16)
                sp.dma_start(xq[0:127, t0 + 7, :], x[b, 897:1024, :]).then_inc(s_xq[b], 16)
                sp.dma_start(xq[127:128, t0 + 7, :], x[b, 0:1, :]).then_inc(s_xq[b], 16)
            for c in range(3):
                sp.dma_start(w_sb[:, c * INNER:(c + 1) * INNER], w_qkv[:, c * INNER:(c + 1) * INNER]).then_inc(s_wqkv[c], 16)
            sp.dma_start(wo_sb[:, :, :], w_out.rearrange("(t p) n -> p t n", p=P)).then_inc(s_wout, 16)
            sp.wait_ge(s_zero, 1)
            for it in (0, 2):
                sp.dma_start(x_rows[it, 0:LEAD, :], zrow[:, :]).then_inc(s_xrows, 16)
            sp.wait_ge(s_xsh, 1)
            sp.wait_ge(s_xsl, 1)
            for it in range(ITERS):
                sp.dma_start(x_rows[it, LEAD:XROWS, :].rearrange("(m p) c -> p m c", p=P),
                             xs[:, TPI * it:TPI * it + TPI, :, :].rearrange("p m s c -> p m (s c)")).then_inc(s_xrows, 16)
                last = (it // 2 + 1) * (NT // B) - 1
                sp.dma_start(bos_rows[it:it + 1, :], xs[127:128, last, :, :].rearrange("p s c -> p (s c)")).then_inc(s_xrows, 16)
            for it in (1, 3):
                sp.dma_start(x_rows[it, 0:LEAD, :], xs[P - LEAD:P, TPI * it - 1, :, :].rearrange("p s c -> p (s c)")).then_inc(s_xrows, 16)
            for i in range(2):
                sp.dma_start(w_ff[:, i, :].rearrange("p (t d) -> p t d", t=FT) if i == 0 else w_ff[:, 1, :],
                             w_up.rearrange("(t p) d -> p t d", p=P) if i == 0 else w_down).then_inc(s_wff, 16)
            sp.wait_ge(s_eva, read_no("A", "p", 3))
            sp.wait_ge(s_evd, read_no("D", "p", 3))
            sp.dma_start(pt_rows.rearrange("g o c -> o g c"), PT[:, :, :]).then_inc(s_pt, 16)
            sp.wait_ge(s_pt, 16)
            sp.dma_start(R[:, :, :], pt_rows.rearrange("g (a b) c -> (g a) b c", a=IL)).then_inc(s_R, 16)
            sp.wait_ge(s_xrows, 16 * (2 + 2 * ITERS + 2))
            with sp.Fori(0, ITERS) as I:
                for par in range(2):
                    sp.wait_ge(s_C, AHEAD_C + 16 * I - 8 + 8 * par)
                    for q in range(2):
                        for a in range(3):
                            m0, s0 = divmod(par * CHUNK + BLK * (q + a), 2 * BLK)
                            rows = x_rows.rearrange("i (m s) c -> i m s c", s=2 * BLK)
                            src = rows[I, m0:m0 + CPAIR, s0:s0 + BLK, :].rearrange("m r c -> r m c")
                            row = 64 * q + SEG * a
                            sp.dma_start(f32(xw[par][row:row + BLK, :, :, :]).rearrange("p m s c -> p m (s c)"),
                                         src).then_inc(s_win[par], 16)
                        row = 64 * q + BLK
                        sp.dma_start(f32(xw[par][row:row + SEG + 1:SEG, :, :, :]).rearrange("p m s c -> p m (s c)"),
                                     bos_rows[I, :].unsqueeze(0).unsqueeze(1).broadcast_to([2, CPAIR, 2 * P])).then_inc(s_win[par], 16)
            flat = out.rearrange("b n c -> (b n) c")
            sp.sem_inc(f_store, AHEAD_STORE)
            with sp.Fori(0, B) as b:
                for half in range(2):
                    sp.wait_ge(f_out, AHEAD_OUT + 8 * b + 4 * half + 4)
                    t = b * N + ITER_TOK * half
                    for m in range(TPI):
                        n = P if m < TPI - 1 else P - 1
                        sp.dma_start(flat[bass.ds(t + 1 + m * P, n), :], outS[0:n, m, :]).then_inc(f_store, 16)
                    sp.dma_start(flat[bass.ds(b * N + (ITER_TOK if half == 0 else 0), 1), :],
                                 outS[P - 1:P, TPI - 1, :]).then_inc(f_store, 16)
            sp.wait_ge(f_store, AHEAD_STORE + 16 * (TPI + 1) * ITERS)

        @block.gpsimd
        def _(pool):
            nc.gpsimd.memset(ident[:, :], 0.0).then_inc(s_pool, 1)
            pool.wait_ge(s_pool, 1)
            nc.gpsimd.affine_select(out=ident[:, :], in_=ident[:, :], compare_op=ALU.not_equal, fill=1.0,
                                    base=0, pattern=[[-1, P]], channel_multiplier=1).then_inc(s_ident, 1)
            nc.gpsimd.memset(zrow[:, :], 0.0).then_inc(s_zero, 1)
            nc.gpsimd.memset(xT17[:, 0:3:2, 0:2, 0:BLK], 0.0).then_inc(s_zero, 1)
            pool.dma_start(b_sb[:, :], b_out.rearrange("(c o) -> c o", o=1)).then_inc(s_small, 16)
            for k in range(IL):
                pool.dma_start(wth8[k:P:IL, :], w_th).then_inc(s_small, 16)
            nc.gpsimd.memset(sel[:, :], 0.0).then_inc(s_const, 1)
            m = mask[:, :, :].rearrange("p v (r f q w) -> p v r f q w", r=2, f=2, q=2)
            nc.gpsimd.memset(mask[:, :, :], 0.0).then_inc(s_mask, 1)
            pool.wait_ge(s_mask, 1)
            n = 1
            for v in range(2):
                for r in range(2):
                    for f in range(2):
                        own = m[0:IL, v, r, f, :, 2 * SEG:WIN]
                        nc.gpsimd.affine_select(out=own, in_=own, compare_op=ALU.is_ge, fill=NEG, base=IL * f,
                                                pattern=[[0, 2], [-1, BLK]], channel_multiplier=1).then_inc(s_mask, 1)
                        n += 1
                        nc.gpsimd.memset(m[0:IL, v, r, f, :, 2 * SEG - 1:2 * SEG], NEG)
            for f in range(2):
                nc.gpsimd.memset(m[0:IL, 0, 0, f, :, 0:BLK], NEG)
                nc.gpsimd.memset(m[0:IL, 0, 0, f, 0, SEG:SEG + BLK], NEG).then_inc(s_mask, 1)
            for i in range(2):
                nc.gpsimd.memset(E[i][:, :, :], 0.0).then_inc(s_epad, 1)
            for c, value in enumerate(CONSTS):
                nc.gpsimd.memset(consts[:, c, :], value)
            pool.wait_ge(s_xsh, 1)
            nc.gpsimd.tensor_tensor(xs[:, :, 1, :], xq[:, :, :], xs[:, :, 0, :], ALU.subtract).then_inc(s_xsl, 1)
            pool.wait_ge(s_wout, 16)
            nc.gpsimd.tensor_copy(wo_p[:, :, :, :], wo_sb[:, :, :].rearrange("p t (b a) -> p t a b", a=IL)).then_inc(s_wop, 1)
            pool.wait_ge(s_asum, 2)
            nc.gpsimd.partition_all_reduce(tsum[:, 2:4], tsum[:, 0:2], P, RADD).then_inc(s_atot, 1)

            with pool.Fori(0, ITERS) as I:
                for j in range(SLOTS):
                    e = E[j % 2][:, :, 0:WIN]
                    pool.wait_ge(s_rec, SLOTS * I + j + 1)
                    nc.gpsimd.tensor_tensor(e, e, rc[j % 2][:, :].unsqueeze(2).broadcast_to([P, TILES, WIN]),
                                            ALU.mult).then_inc(s_norm, 1)

            tt = nc.gpsimd.tensor_tensor

            pool.sem_inc(f_hrms, AHEAD_HRMS)
            pool.sem_inc(f_out, AHEAD_OUT)
            with pool.Fori(0, ITERS + 1) as g:
                with pool.If(g < ITERS):
                    pool.wait_ge(f_var, 4 * g + 4)
                    tt(tiny[:, 0, :], mv[:, :, 1], consts[:, C_EPS_LN, :], ALU.add).then_inc(f_eps, 1)
                    pool.wait_ge(f_eps, g + 1)
                    tt(rstd[:, :], tiny[:, 0, :], consts[:, MINUS_HALF, :], ALU.pow).then_inc(f_rstd, 1)
                    tt(tiny[:, 1, :], mv[:, :, 1], consts[:, HALF, :], ALU.pow).then_inc(f_rms, 1)
                    pool.wait_ge(f_rms, 3 * g + 1)
                    pool.wait_ge(f_rstd, g + 1)
                    tt(tiny[:, 2, :], tiny[:, 1, :], rstd[:, :], ALU.mult).then_inc(f_rms, 1)
                    pool.wait_ge(f_rms, 3 * g + 2)
                    tt(tiny[:, 3, :], tiny[:, 2, :], consts[:, C_EPS_RMS, :], ALU.add).then_inc(f_rms, 1)
                    pool.wait_ge(f_rms, 3 * g + 3)
                    tt(inv[:, bass.ds(g % ITERS * TPI, TPI)], tiny[:, 3, :], consts[:, MINUS_ONE, :], ALU.pow).then_inc(f_inv, 1)
                    pool.wait_ge(f_x1, 4 * g + 4)
                    nc.gpsimd.tensor_copy(x1all[:, bass.ds(g % ITERS * TPI, TPI), :], x1[:, :, :]).then_inc(f_x1c, 1)
                with pool.If(g > 0):
                    pool.wait_ge(f_sq, AHEAD_SQ + 4 * g)
                    tt(tiny[:, 4, :], hss[:, :], consts[:, C_PER_FF, :], ALU.mult).then_inc(f_hrms, 1)
                    pool.wait_ge(f_hrms, AHEAD_HRMS + 3 * g - 2)
                    tt(tiny[:, 5, :], tiny[:, 4, :], consts[:, HALF, :], ALU.pow).then_inc(f_hrms, 1)
                    pool.wait_ge(f_hrms, AHEAD_HRMS + 3 * g - 1)
                    tt(tiny[:, 6, :], tiny[:, 5, :], consts[:, C_EPS_RMS, :], ALU.add).then_inc(f_hrms, 1)
                    pool.wait_ge(f_hrms, AHEAD_HRMS + 3 * g)
                    tt(hinv[:, :], tiny[:, 6, :], consts[:, MINUS_ONE, :], ALU.pow).then_inc(f_hinv, 1)
                    pool.wait_ge(f_var2, 4 * g)
                    tt(tiny[:, 7, :], mv2[:, :, 1], consts[:, C_EPS_LN, :], ALU.add).then_inc(f_eps2, 1)
                    pool.wait_ge(f_eps2, g)
                    tt(rstd2[:, :], tiny[:, 7, :], consts[:, MINUS_HALF, :], ALU.pow).then_inc(f_rstd2, 1)
                    pool.wait_ge(f_store, AHEAD_STORE + 16 * (TPI + 1) * (g - 1))
                    pool.sem_inc(f_seen_pool, 1)
                    pool.wait_ge(f_rstd2, g)
                    pool.sem_inc(f_seen_pool, 1)
                    for i in range(TPI):
                        nc.gpsimd.tensor_scalar(outS[:, i, :], y2[:, i, :], mv2[:, i, 0:1], rstd2[:, i:i + 1],
                                                ALU.subtract, ALU.mult).then_inc(f_out, 1)

        @block.scalar
        def _(act):
            copy = lambda o, i, **k: nc.scalar.activation(o, i, ACT.Copy, **k)
            def fills(fs):
                for kind, i, bk, who in fs:
                    if "A" not in who:
                        continue
                    act.wait_ge(s_fill, fill_no(kind, i))
                    if kind == "x":
                        copy(xTh[:, 512 * i:512 * (i + 1)], bank[bk][:, :]).then_inc(s_eva, 1)
                        if i == 3:
                            copy(xs[:, :, 0, :].bitcast(F32R), xq[:, :, :]).then_inc(s_xsh, 1)
                    elif kind == "w":
                        copy(wT[:, 4 * i:4 * i + 4, :], bank[bk][:, :].rearrange("p (t c) -> p t c", t=4)).then_inc(s_eva, 1)
                    elif kind == "g":
                        hs = heads(i)
                        copy(Gh[:, hs[0]:hs[-1] + 1:2, :], bank[bk][:, :].rearrange("p (t c) -> p t c", t=4),
                             scale=SCALE).then_inc(s_eva, 1)
                    elif kind == "p":
                        hs = heads(i)
                        copy(PT[:, hs[0]:hs[-1] + 1:2, :], bank[bk][:, :].rearrange("p (t c) -> p t c", t=4)).then_inc(s_eva, 1)
                    elif kind == "m":
                        o = Mh[:, :, 32 * i:32 * i + 32].rearrange("p h (a b) -> p a h b", b=IL)
                        copy(o, bank[bk][:, :].rearrange("p (a h b) -> p a h b", a=4, b=IL)).then_inc(s_eva, 1)
                    elif kind == "t":
                        copy(wuT[:, :], bank[bk][:, :]).then_inc(s_eva, 1)

            fills(FILLS)
            for b in range(8):
                act.wait_ge(s_Y, b + 1)
                copy(Y_out(b, 0, 2 * b), bank[Y_BANK[b % 2]][:, :].rearrange("p (h t i) -> p h t i", h=2, i=IL)).then_inc(s_Ye, 1)
            fills(TAIL)

            def ct_hi(j, t2):
                sc, par = (j - 2) % 4, ((j - 2) // 4) % 2
                for bk in range(2):
                    act.wait_ge(s_C, AHEAD_C + t2 + 1 + bk)
                    copy(ct_view(CTh[par], sc, bk), c_view(bk)).then_inc(s_CTh, 1)

            def at_hi(j, t):
                act.wait_ge(s_T, t)
                copy(ATh[(j - 1) % 2][:, :], bank[T_BANK][:, :]).then_inc(s_ATh, 1)

            act.sem_inc(s_CTh, AHEAD_CT)
            act.sem_inc(s_Oe, AHEAD_OE)
            with act.Fori(0, ITERS) as I:
                for j in range(SLOTS):
                    if j == 2:
                        act.wait_ge(s_O, AHEAD_O + 2 * I - 1)
                    if j == 6:
                        act.wait_ge(s_O, AHEAD_O + 2 * I)
                    with since(act, I, j, 2):
                        ct_hi(j, 16 * I + 2 * j - 4)
                    with since(act, I, j, 1):
                        at_hi(j, SLOTS * I + j)

                    def y_out(b):
                        with before_last(act, I, j):
                            if j % 4 == 0 and b == 0:
                                act.wait_ge(s_S, SLOTS * I + j)
                            act.wait_ge(s_Y, 16 * I + 2 * j + b + 9)
                            copy(Y_out(b, (j // 4 + 1) % 2, 4 * (j % 4) + 2 * b),
                                 bank[Y_BANK[b]][:, :].rearrange("p (h t i) -> p h t i", h=2, i=IL)).then_inc(s_Ye, 1)
                    y_out(0)
                    e = E[j % 2][:, :, 0:WIN]
                    act.wait_ge(s_sub, AHEAD_SUB + SLOTS * I + j + 1)
                    nc.scalar.activation(e, e, ACT.Exp).then_inc(s_exp, 1)
                    y_out(1)
                    if j in (0, 4):
                        with act.If(I > 0):
                            act.wait_ge(s_O, AHEAD_O + 2 * I - 1 + j // 4)
                            copy(attnT[:, bass.ds((2 * I + 2 * ITERS - 2 + j // 4) % (2 * ITERS) * CHUNK, CHUNK)],
                                 bank[O_BANK][:, 0:CHUNK]).then_inc(s_Oe, 1)
            last = SLOTS * ITERS
            ct_hi(0, 2 * last - 4)
            at_hi(0, last)
            act.wait_ge(s_O, AHEAD_O + 2 * ITERS - 1)
            copy(attnT[:, (2 * ITERS - 2) * CHUNK:(2 * ITERS - 1) * CHUNK], bank[O_BANK][:, 0:CHUNK]).then_inc(s_Oe, 1)
            ct_hi(1, 2 * last - 2)
            act.wait_ge(s_O, AHEAD_O + 2 * ITERS)
            copy(attnT[:, (2 * ITERS - 1) * CHUNK:2 * ITERS * CHUNK], bank[O_BANK][:, 0:CHUNK]).then_inc(s_Oe, 1)

            def x1_hi(g):
                act.wait_ge(f_up, 4 * g)
                act.wait_ge(f_xT, g + 1)
                copy(x1Th[:, :], bank[1][:, :]).then_inc(f_xTh, 1)

            def gelu(g, i):
                act.wait_ge(f_up, 4 * g + i + 1)
                act.wait_ge(f_hT, AHEAD_HT + 4 * g + i - 1)
                act.wait_ge(f_sq, AHEAD_SQ + 4 * g + i - 1)
                act.sem_inc(f_seen_act, 1)
                nc.scalar.activation(gS[i % 2][:, :], bank[2 + i % 2][:, :], ACT.Gelu,
                                     scale=inv[:, bass.ds(g * TPI + i, 1)]).then_inc(f_gelu, 1)

            def squares(g, i):
                act.wait_ge(f_gelu, AHEAD_GELU + 4 * g + i + 1)
                act.wait_ge(f_sq, AHEAD_SQ + 4 * g + i)
                nc.scalar.activation(sq[:, :], gS[i % 2][:, :], ACT.Square, accum_out=hss[:, i:i + 1]).then_inc(f_sq, 1)

            def h_hi(g, i):
                act.wait_ge(f_hT, AHEAD_HT + 4 * g + i + 1)
                copy(hTh[:, :, P * i:P * i + P], bank[4 + i % 2][:, :].rearrange("p (t c) -> p t c", t=FT)).then_inc(f_hTh, 1)

            act.sem_inc(f_gelu, AHEAD_GELU)
            act.sem_inc(f_sq, AHEAD_SQ)
            x1_hi(0)
            with act.Fori(0, ITERS) as g:
                act.wait_ge(f_inv, g + 1)
                act.sem_inc(f_seen_act, 1)
                gelu(g, 0)
                gelu(g, 1)
                act.wait_ge(f_hinv, g)
                squares(g, 0)
                act.wait_ge(f_dn, g)
                h_hi(g, 0)
                gelu(g, 2)
                squares(g, 1)
                h_hi(g, 1)
                gelu(g, 3)
                squares(g, 2)
                h_hi(g, 2)
                squares(g, 3)
                h_hi(g, 3)
                with act.If(g < ITERS - 1):
                    x1_hi(g + 1)
                act.wait_ge(f_dn, g + 1)
                act.wait_ge(f_back, g)
                copy(dS[:, :], bank[6][:, :]).then_inc(f_dnE, 1)

        @block.vector
        def _(dve):
            v = nc.vector
            dve.wait_ge(s_ident, 1)
            v.tensor_reduce(sel8[:, :], ident[:, :].rearrange("p (g k) -> p k g", k=IL), AX.X, ALU.add).then_inc(s_sel8, 1)
            dve.wait_ge(s_const, 1)
            v.tensor_copy(sel[0:IL, :].rearrange("p (h k) -> p h k", k=IL),
                          ident[0:IL, 0:IL].unsqueeze(1).broadcast_to([IL, H, IL])).then_inc(s_sel, 1)

            def fills(fs):
                for kind, i, bk, who in fs:
                    if "D" not in who:
                        continue
                    dve.wait_ge(s_fill, fill_no(kind, i))
                    if kind == "x":
                        dve.wait_ge(s_eva, read_no("A", kind, i))
                        v.tensor_copy(xT17[:, i, 2:IBLK + 2, 0:BLK], bank[bk][:, :].rearrange("p (u s) -> p u s", s=BLK))
                        if i % 2 == 0:
                            v.tensor_copy(xT17[:, i + 1, 0:2, 0:BLK],
                                          bank[bk][:, 512 - LEAD:512].rearrange("p (u s) -> p u s", s=BLK))
                        else:
                            v.tensor_copy(xT17[:, i - 1:i + 1, :, BLK],
                                          bank[bk][:, 511:512].unsqueeze(2).broadcast_to([P, 2, IBLK + 2]))
                        o = slice(512 * i, 512 * (i + 1))
                        v.tensor_tensor(xTl[:, o], bank[bk][:, :], f32(xTh[:, o]), ALU.subtract).then_inc(s_evd, 1)
                    elif kind == "w":
                        v.tensor_copy(wT[:, 4 * i:4 * i + 4, :], bank[bk][:, :].rearrange("p (t c) -> p t c", t=4)).then_inc(s_evd, 1)
                    elif kind == "g":
                        hs = heads(i)
                        o = slice(hs[0], hs[-1] + 1, 2)
                        dve.wait_ge(s_eva, read_no("A", kind, i))
                        v.scalar_tensor_tensor(out=Gl[:, o, :], in0=bank[bk][:, :].rearrange("p (t c) -> p t c", t=4),
                                               scalar=SCALE, in1=f32(Gh[:, o, :]), op0=ALU.mult,
                                               op1=ALU.subtract).then_inc(s_evd, 1)
                    elif kind == "p":
                        hs = heads(i)
                        v.tensor_copy(PT[:, hs[0]:hs[-1] + 1:2, :], bank[bk][:, :].rearrange("p (t c) -> p t c", t=4)).then_inc(s_evd, 1)
                    elif kind == "m":
                        o = slice(32 * i, 32 * i + 32)
                        dve.wait_ge(s_eva, read_no("A", kind, i))
                        v.tensor_tensor(Ml[:, :, o].rearrange("p h (a b) -> p a h b", b=IL),
                                        bank[bk][:, :].rearrange("p (a h b) -> p a h b", a=4, b=IL),
                                        f32(Mh[:, :, o]).rearrange("p h (a b) -> p a h b", b=IL),
                                        ALU.subtract).then_inc(s_evd, 1)
                    elif kind == "t":
                        v.tensor_copy(wdT[:, :, :], bank[bk][:, :].rearrange("p (t c) -> p t c", t=4)).then_inc(s_evd, 1)
                    elif kind == "v0":
                        v.tensor_copy(v0T[:, :], bank[bk][:, 0:16]).then_inc(s_evd, 1)
                    elif kind == "bos":
                        v.tensor_copy(bosT[:, :], bank[bk][:, 0:B]).then_inc(s_evd, 1)

            fills(FILLS)
            dve.wait_ge(s_small, 16 * (IL + 1))
            dve.wait_ge(s_sel8, 1)
            v.tensor_tensor(kron[:, :].rearrange("p (h k) -> p h k", k=IL),
                            wth8[:, :].unsqueeze(2).broadcast_to([P, H, IL]),
                            sel8[:, :].unsqueeze(1).broadcast_to([P, H, IL]), ALU.mult).then_inc(s_kron, 1)
            dve.wait_ge(s_wff, 32)
            for k in range(2):
                v.tensor_reduce(tsum[:, k:k + 1], w_ff[:, k, :], AX.X, ALU.add, apply_absolute_value=True).then_inc(s_asum, 1)
            dve.wait_ge(s_atot, 1)
            v.tensor_scalar(tsum[:, 4:6], tsum[:, 2:4], 1.0 / (FF * D), 0.5, ALU.mult, ALU.mult).then_inc(s_thr, 1)
            v.tensor_scalar(tsum[:, 6:8], tsum[:, 2:4], 1.0 / (FF * D), -0.5, ALU.mult, ALU.mult).then_inc(s_thr, 1)
            dve.wait_ge(s_thr, 2)
            for k in range(2):
                v.tensor_scalar(tern[:, k, :], w_ff[:, k, :], tsum[:, 6 + k:7 + k], None, ALU.is_lt).then_inc(s_ternd, 1)
            dve.wait_ge(s_ternd, 2)
            for k in range(2):
                v.scalar_tensor_tensor(out=w_ff[:, k, :], in0=w_ff[:, k, :], scalar=tsum[:, 4 + k:5 + k],
                                       in1=tern[:, k, :], op0=ALU.is_gt, op1=ALU.subtract).then_inc(s_tern, 1)
            fills(TAIL)

            def ct_lo(j, t2):
                sc, par = (j - 2) % 4, ((j - 2) // 4) % 2
                for bk in range(2):
                    dve.wait_ge(s_CTh, AHEAD_CT + t2 + 1 + bk)
                    v.tensor_tensor(ct_view(CTl[par], sc, bk), c_view(bk), ct_view(f32(CTh[par][:, :, :]), sc, bk),
                                    ALU.subtract).then_inc(s_CTl, 1)

            def at_lo(j, t):
                dve.wait_ge(s_ATh, t)
                v.tensor_tensor(ATl[(j - 1) % 2][:, :], bank[T_BANK][:, :], f32(ATh[(j - 1) % 2][:, :]),
                                ALU.subtract).then_inc(s_ATl, 1)

            dve.sem_inc(s_CTl, AHEAD_CT)
            dve.sem_inc(s_sub, AHEAD_SUB)
            dve.sem_inc(s_ATl, AHEAD_ATL)
            with dve.Fori(0, ITERS) as I:
                for j in range(SLOTS):
                    k = j % 2
                    with since(dve, I, j, 2):
                        ct_lo(j, 16 * I + 2 * j - 4)
                    with since(dve, I, j, 1):
                        at_lo(j, SLOTS * I + j)
                    s = bank[S_BANK[k]][:, 0:TILES * WIN].rearrange("p (t w) -> p t w", w=WIN)
                    e = E[k][:, :, 0:WIN]
                    dve.wait_ge(s_S, SLOTS * I + j + 1)
                    v.tensor_reduce(mx[k][:, :], s, AX.X, ALU.max).then_inc(s_max, 1)
                    dve.wait_ge(s_max, SLOTS * I + j + 1)
                    v.tensor_tensor(e, s, mx[k][:, :].unsqueeze(2).broadcast_to([P, TILES, WIN]),
                                    ALU.subtract).then_inc(s_sub, 1)
                    dve.wait_ge(s_exp, SLOTS * I + j + 1)
                    v.tensor_reduce(sm[k][:, :], e, AX.X, ALU.add).then_inc(s_sum, 1)
                    dve.wait_ge(s_sum, SLOTS * I + j + 1)
                    v.reciprocal(rc[k][:, :], sm[k][:, :]).then_inc(s_rec, 1)
            last = SLOTS * ITERS
            ct_lo(0, 2 * last - 4)
            at_lo(0, last)
            ct_lo(1, 2 * last - 2)

            dve.wait_ge(s_Oe, AHEAD_OE + 2 * ITERS)
            for b in range(B):
                v.tensor_copy(attnT[:, b * N + N - 1:b * N + N], bosT[:, b:b + 1]).then_inc(f_bosput, 1)
            dve.wait_ge(f_bosput, B)

            def stage(g):
                dve.wait_ge(f_aT, g)
                v.tensor_scalar(attnS[:, :], attnT[:, bass.ds(g % ITERS * ITER_TOK, ITER_TOK)], b_sb[:, 0:1], None,
                                ALU.add).then_inc(f_stage, 1)

            def residual(g):
                dve.wait_ge(f_aT, g + 1)
                v.tensor_tensor(res[:, :, :], bank[0][:, :].rearrange("p (t c) -> p t c", t=TPI),
                                xq[:, bass.ds(g % ITERS * TPI, TPI), :], ALU.add).then_inc(f_res, 1)
                dve.wait_ge(f_res, g + 1)
                for i in range(TPI):
                    v.bn_stats(st[:, i, :], res[:, i, :]).then_inc(f_st, 1)
                dve.wait_ge(f_inv, g)
                dve.wait_ge(f_st, 4 * g + 4)
                dve.sem_inc(f_seen, 1)
                for i in range(TPI):
                    v.bn_aggr(mv[:, i, :], st[:, i, :]).then_inc(f_var, 1)

            def layernorm(g):
                dve.wait_ge(f_xT, g)
                dve.wait_ge(f_x1c, g)
                dve.wait_ge(f_rstd, g + 1)
                for i in range(TPI):
                    v.tensor_scalar(x1[:, i, :], res[:, i, :], mv[:, i, 0:1], rstd[:, i:i + 1], ALU.subtract,
                                    ALU.mult).then_inc(f_x1, 1)

            def x1_lo(g):
                dve.wait_ge(f_xTh, g + 1)
                v.tensor_tensor(x1Tl[:, :], bank[1][:, :], f32(x1Th[:, :]), ALU.subtract).then_inc(f_xTl, 1)

            def h_lo(g, i):
                dve.wait_ge(f_hTh, 4 * g + i + 1)
                c = slice(P * i, P * i + P)
                v.tensor_tensor(hTl[:, :, c], bank[4 + i % 2][:, :].rearrange("p (t c) -> p t c", t=FT),
                                f32(hTh[:, :, c]), ALU.subtract).then_inc(f_hTl, 1)

            def second(g):
                dve.wait_ge(f_back, g)
                dve.wait_ge(f_hinv, g)
                dve.wait_ge(f_out, AHEAD_OUT + 4 * g - 4)
                for i in range(TPI):
                    v.scalar_tensor_tensor(out=y2[:, i:i + 1, :], in0=bank[7][:, P * i:P * i + P].unsqueeze(1),
                                           scalar=hinv[:, i:i + 1], in1=x1all[:, bass.ds((g + ITERS - 1) % ITERS * TPI + i, 1), :],
                                           op0=ALU.mult, op1=ALU.add).then_inc(f_y2, 1)
                for i in range(TPI):
                    dve.wait_ge(f_y2, AHEAD_Y2 + 4 * g - 3 + i)
                    v.bn_stats(st2[:, i, :], y2[:, i, :]).then_inc(f_st2, 1)
                dve.wait_ge(f_st2, 4 * g)
                dve.sem_inc(f_seen, 1)
                for i in range(TPI):
                    v.bn_aggr(mv2[:, i, :], st2[:, i, :]).then_inc(f_var2, 1)

            dve.sem_inc(f_hTl, AHEAD_HTL)
            dve.sem_inc(f_y2, AHEAD_Y2)
            stage(0)
            residual(0)
            layernorm(0)
            x1_lo(0)
            with dve.Fori(0, ITERS) as g:
                with dve.If(g < ITERS - 1):
                    stage(g + 1)
                with dve.If(g > 0):
                    second(g)
                with dve.If(g < ITERS - 1):
                    residual(g + 1)
                h_lo(g, 0)
                with dve.If(g < ITERS - 1):
                    layernorm(g + 1)
                for i in range(1, TPI):
                    h_lo(g, i)
                with dve.If(g < ITERS - 1):
                    x1_lo(g + 1)
            second(ITERS)

        @block.tensor
        def _(pe):
            mm = nc.tensor.matmul

            def split3(o, wh, wl, rh, rl, start=True, stop=True, **k):
                mm(o, wh, rh, start=start, stop=False, **k)
                mm(o, wh, rl, start=False, stop=False, **k)
                return mm(o, wl, rh, start=False, stop=stop, **k)

            def y_part(bk, chunk_cols, h0):
                for n in range(2):
                    ins = split3(bank[Y_BANK[bk]][:, CHUNK * n:CHUNK * (n + 1)], Gh[:, h0 + n, :], Gl[:, h0 + n, :],
                                 xTh[:, chunk_cols], xTl[:, chunk_cols])
                ins.then_inc(s_Y, 1)

            def fills(fs):
                for kind, i, bk, who in fs:
                    bank_free(pe, kind, i)
                    bnk = bank[bk]
                    if kind == "x":
                        if i % 2 == 0:
                            pe.wait_ge(s_ident, 1)
                            pe.wait_ge(s_xq[i // 2], 48)
                        for k in range(4):
                            ins = nc.tensor.transpose(bnk[:, P * k:P * k + P], xq[:, 4 * i + k, :], ident[:, :])
                    elif kind == "w":
                        pe.wait_ge(s_wqkv[i // 2], 16)
                        for k in range(4):
                            c = P * (4 * i + k)
                            ins = nc.tensor.transpose(bnk[:, P * k:P * k + P], w_sb[:, c:c + P], ident[:, :])
                    elif kind == "g":
                        if i == 0:
                            for n in range(4):
                                pe.wait_ge(s_eva if n % 2 == 0 else s_evd, read_no("AD"[n % 2], "w", n))
                        for k, h in enumerate(heads(i)):
                            r = slice(DH * (h % 2), DH * (h % 2) + DH)
                            ins = mm(bnk[:, P * k:P * k + P], wT[r, h // 2, :], wT[r, 8 + h // 2, :], start=True, stop=True)
                    elif kind == "p":
                        if i == 0:
                            pe.wait_ge(s_wop, 1)
                            for n in (4, 5):
                                pe.wait_ge(s_eva if n % 2 == 0 else s_evd, read_no("AD"[n % 2], "w", n))
                        for k, h in enumerate(heads(i)):
                            r = slice(DH * (h % 2), DH * (h % 2) + DH)
                            o = wo_p[r, h // 2, :, :].rearrange("p a b -> p (a b)")
                            ins = mm(bnk[:, P * k:P * k + P], o, wT[r, 16 + h // 2, :], start=True, stop=True)
                    elif kind == "m":
                        if i == 0:
                            pe.wait_ge(s_R, 16)
                            pe.wait_ge(s_kron, 1)
                        for k in range(4):
                            ins = mm(bnk[:, P * k:P * k + P], R[:, 4 * i + k, :], kron[:, :], start=True, stop=True)
                    elif kind == "t":
                        pe.wait_ge(s_tern, 2)
                        for k in range(4):
                            ins = nc.tensor.transpose(bnk[:, P * k:P * k + P], w_ff[:, i, P * k:P * k + P], ident[:, :])
                    elif kind == "v0":
                        for k in range(8):
                            c = 2 * INNER + P * k
                            ins = mm(bnk[:, 2 * k:2 * k + 2], w_sb[:, c:c + P], xT17[:, 0:3:2, 0, BLK], start=True, stop=True)
                    elif kind == "bos":
                        pe.wait_ge(s_evd, read_no("D", "v0", 0))
                        for k in range(8):
                            ins = mm(bnk[:, 0:2], wo_sb[:, k, :], v0T[:, 2 * k:2 * k + 2], start=(k == 0), stop=(k == 7))
                    ins.then_inc(s_fill, 1)

            fills(FILLS)
            pe.wait_ge(s_eva, read_no("A", "g", 3))
            pe.wait_ge(s_evd, read_no("D", "g", 3))
            for b in range(8):
                if b >= 2:
                    pe.wait_ge(s_Ye, b - 1)
                y_part(b % 2, slice(0, CHUNK), 2 * b)
            fills(TAIL)
            pe.wait_ge(s_eva, read_no("A", "bos", 0))
            pe.wait_ge(s_evd, read_no("D", "bos", 0))
            pe.wait_ge(s_zero, 2)
            pe.wait_ge(s_mask, MASKS)
            pe.wait_ge(s_sel, 1)

            def transposes(j, t):
                pe.wait_ge(s_norm, t)
                for r in range(2):
                    for f in range(2):
                        o = bank[T_BANK][:, 256 * r:256 * r + 256].rearrange("p (h s) -> p h s", s=BLK)
                        k = 4 * r + 2 * f
                        ins = nc.tensor.transpose(o[:, :, IL * f:IL * f + IL],
                                                  E[(j - 1) % 2][:, k:k + 2, :].rearrange("p t w -> p (t w)"), ident[:, :])
                ins.then_inc(s_T, 1)

            def c_part(j):
                sc, par, k = (j - 1) % 4, ((j - 1) // 4) % 2, (j - 1) % 2
                for r in range(2):
                    ins = []
                    for q in range(2):
                        row, col = slice(64 * q, 64 * q + WIN), slice(256 * r, 256 * r + 256)
                        m = 2 * sc + r
                        ins.append(split3(bank[C_BANK[q]][:, col], xw[par][row, m, 0, :], xw[par][row, m, 1, :],
                                          ATh[k][row, col], ATl[k][row, col]))
                for i in ins:
                    i.then_inc(s_C, 1)

            def o_part(p, par):
                for h in range(4 * p, 4 * p + 4):
                    ins = split3(bank[O_BANK][:, 0:CHUNK], Mh[:, h, :], Ml[:, h, :], CTh[par][:, h, :], CTl[par][:, h, :],
                                 start=(h == 0), stop=(h == H - 1))
                if p == 3:
                    ins.then_inc(s_O, 1)

            pe.sem_inc(s_C, AHEAD_C)
            pe.sem_inc(s_O, AHEAD_O)
            with pe.Fori(0, ITERS) as I:
                for j in range(SLOTS):
                    k = j % 2
                    with since(pe, I, j, 1):
                        pe.wait_ge(s_ATl, AHEAD_ATL + SLOTS * I + j - 1)
                        transposes(j, SLOTS * I + j)
                    pe.wait_ge(s_sub, AHEAD_SUB + SLOTS * I + j - 1)
                    if j % 4 == 0:
                        pe.wait_ge(s_Ye, 16 * I + 2 * j + 8)
                    v = bass.ds(I % 2, 1) if j == 0 else slice(1, 2)
                    mm(bank[S_BANK[k]][:, 0:TILES * WIN], sel[:, :], mask[:, v, :].rearrange("p a w -> p (a w)"),
                       start=True, stop=False)
                    for tile in range(TILES):
                        r, f, q = tile // 4, tile // 2 % 2, tile % 2
                        blk = STEP_BLK * j + 2 * r + q
                        ytile = 2 * (blk % CBLK) + f
                        keys = xT17[:, bass.ds(I, 1), :, :].rearrange("p i u s -> p (i u s)")[:, SEG * blk:SEG * blk + WIN]
                        ins = mm(bank[S_BANK[k]][:, WIN * tile:WIN * tile + WIN], Yb[(j // 4) % 2][:, ytile, :], keys,
                                 start=False, stop=(tile == TILES - 1))
                    ins.then_inc(s_S, 1)
                    with before_last(pe, I, j):
                        for b in range(2):
                            pe.wait_ge(s_Ye, 16 * I + 2 * j + b + 7)
                            y_part(b, bass.ds((2 * I + j // 4 + 1) % (2 * ITERS) * CHUNK, CHUNK), 4 * (j % 4) + 2 * b)
                    with since(pe, I, j, 5):
                        n, p = divmod(j + 3, 4)
                        if p == 0:
                            pe.wait_ge(s_CTl, AHEAD_CT + 8 * (2 * I + n - 1))
                            pe.wait_ge(s_Oe, AHEAD_OE + 2 * I + n - 2)
                        o_part(p, n % 2)
                    with since(pe, I, j, 1):
                        pe.wait_ge(s_ATl, AHEAD_ATL + SLOTS * I + j)
                        pe.wait_ge(s_CTl, AHEAD_CT + 16 * I + 2 * j - 2)
                        if j in (1, 5):
                            pe.wait_ge(s_win[j // 4], 16 * WDMAS * (I + 1))
                        c_part(j)
            last = SLOTS * ITERS
            pe.wait_ge(s_ATl, AHEAD_ATL + last - 1)
            transposes(0, last)
            o_part(3, 0)
            pe.wait_ge(s_ATl, AHEAD_ATL + last)
            pe.wait_ge(s_CTl, AHEAD_CT + 2 * last - 2)
            c_part(0)
            pe.wait_ge(s_CTl, AHEAD_CT + 2 * last)
            pe.wait_ge(s_Oe, AHEAD_OE + 2 * ITERS - 1)
            for p in range(4):
                o_part(p, 1)

            def attn_back(g):
                pe.wait_ge(f_res, g)
                pe.wait_ge(f_stage, g + 1)
                for i in range(TPI):
                    ins = nc.tensor.transpose(bank[0][:, P * i:P * i + P], attnS[:, P * i:P * i + P], ident[:, :])
                ins.then_inc(f_aT, 1)

            def x1_T(g):
                pe.wait_ge(f_xTl, g)
                for i in range(TPI):
                    pe.wait_ge(f_x1, 4 * g + i + 1)
                    ins = nc.tensor.transpose(bank[1][:, P * i:P * i + P], x1[:, i, :], ident[:, :])
                ins.then_inc(f_xT, 1)

            def up(g, i):
                c = slice(P * i, P * i + P)
                pe.wait_ge(f_gelu, AHEAD_GELU + 4 * g + i - 1)
                mm(bank[2 + i % 2][:, :], x1Th[:, c], wuT[:, :], start=True, stop=False)
                mm(bank[2 + i % 2][:, :], x1Tl[:, c], wuT[:, :], start=False, stop=True).then_inc(f_up, 1)

            def h_T(g, i):
                pe.wait_ge(f_gelu, AHEAD_GELU + 4 * g + i + 1)
                pe.wait_ge(f_hTl, AHEAD_HTL + 4 * g + i - 1)
                for k in range(FT):
                    ins = nc.tensor.transpose(bank[4 + i % 2][:, P * k:P * k + P], gS[i % 2][:, P * k:P * k + P], ident[:, :])
                ins.then_inc(f_hT, 1)

            def down(g):
                pe.wait_ge(f_hTl, AHEAD_HTL + 4 * g + 4)
                pe.wait_ge(f_dnE, g)
                for k in range(FT):
                    mm(bank[6][:, :], wdT[:, k, :], hTh[:, k, :], start=(k == 0), stop=False)
                    ins = mm(bank[6][:, :], wdT[:, k, :], hTl[:, k, :], start=False, stop=(k == FT - 1))
                ins.then_inc(f_dn, 1)

            def down_back(g):
                pe.wait_ge(f_dnE, g)
                pe.wait_ge(f_y2, AHEAD_Y2 + 4 * g - 4)
                for i in range(TPI):
                    ins = nc.tensor.transpose(bank[7][:, P * i:P * i + P], dS[:, P * i:P * i + P], ident[:, :])
                ins.then_inc(f_back, 1)

            pe.sem_inc(f_hT, AHEAD_HT)
            attn_back(0)
            x1_T(0)
            with pe.Fori(0, ITERS) as g:
                with pe.If(g < ITERS - 1):
                    attn_back(g + 1)
                pe.wait_ge(f_xTl, g + 1)
                up(g, 0)
                up(g, 1)
                with pe.If(g > 0):
                    down_back(g)
                h_T(g, 0)
                up(g, 2)
                h_T(g, 1)
                up(g, 3)
                h_T(g, 2)
                h_T(g, 3)
                with pe.If(g < ITERS - 1):
                    x1_T(g + 1)
                down(g)
            down_back(ITERS)


_INS = ["L0_attn_x", "L0_attn_w_qkv", "L0_attn_w_out", "L0_attn_b_out", "L0_attn_w_th", "L0_ffn_w_up", "L0_ffn_w_down"]


def kernel(**inputs):
    import numpy as np
    import concourse.bacc as bacc
    from concourse.bass_utils import run_bass_kernel_spmd

    nc = bacc.Bacc("TRN2", target_bir_lowering=False, num_devices=1)
    arrays, args = {}, []
    for name in _INS:
        a = np.ascontiguousarray(inputs[name])
        arrays[f"in_{name}"] = a
        args.append(nc.dram_tensor(f"in_{name}", a.shape, mybir.dt.from_np(a.dtype), kind="ExternalInput").ap())
    out = nc.dram_tensor("out", (B, N, D), F32, kind="ExternalOutput").ap()
    x_rows = nc.dram_tensor("x_rows", (ITERS, XROWS, 2 * D), F32, kind="Internal").ap()
    bos_rows = nc.dram_tensor("bos_rows", (ITERS, 2 * D), F32, kind="Internal").ap()
    pt_rows = nc.dram_tensor("pt_rows", (H, P, P), F32, kind="Internal").ap()
    attention_ffn(nc, *args, out, x_rows, bos_rows, pt_rows)
    r = run_bass_kernel_spmd(nc, [arrays], core_ids=[0])
    return r.results[0]["out"]
```

```python
import concourse.bass as bass
from concourse import mybir
from contextlib import ExitStack, nullcontext

F32 = mybir.dt.float32
F32R = mybir.dt.float32r
BF16 = mybir.dt.bfloat16
ALU = mybir.AluOpType
ACT = mybir.ActivationFunctionType
AX = mybir.AxisListType
RADD = bass.bass_isa.ReduceOp.add

B, N, D = 2, 1024, 128
H, DH = 16, 64
INNER = H * DH
FF = 512
P = 128
BLK = 16
SEG = BLK + 1
WIN = 3 * SEG - 1
PITCH = 64
IL = 8
ITER_TOK = 512
ITERS = B * N // ITER_TOK
IBLK = ITER_TOK // BLK
CHUNK = 256
CBLK = CHUNK // BLK
CPAIR = CBLK // 2
STEP_BLK = 4
SLOTS = IBLK // STEP_BLK
TILES = 2 * STEP_BLK
NEG = -float(2.0 ** 100)
XCOLS = (IBLK + 2) * SEG
LEAD = 2 * BLK
XROWS = LEAD + ITER_TOK
SCALE = float(DH) ** -0.5
EPS_LN, EPS_RMS = 1e-5, 1e-8
TPI = ITER_TOK // P
NT = B * N // P
FT = FF // P
CONSTS = (-0.5, 0.5, -1.0, EPS_LN, EPS_RMS, 1.0 / FF)
MINUS_HALF, HALF, MINUS_ONE, C_EPS_LN, C_EPS_RMS, C_PER_FF = range(6)


def attention_ffn(nc, x, w_qkv, w_out, b_out, w_th, w_up, w_down, out, x_rows, bos_rows, pt_rows):
    ctx = ExitStack()
    with ctx:
        def sb(name, shape, dt=F32):
            return ctx.enter_context(nc.sbuf_tensor(name, shape, dt))

        def sem(name):
            return ctx.enter_context(nc.semaphore(name))

        ident = sb("ident", [P, P])
        sel = sb("sel", [P, P], BF16)
        mask = sb("mask", [P, 2, TILES * WIN], BF16)
        sel8 = sb("sel8", [P, IL])
        wth8 = sb("wth8", [P, H])
        kron = sb("kron", [P, P])
        zrow = sb("zrow", [LEAD, 3 * P])
        tsum = sb("tsum", [P, 8])
        v0T = sb("v0T", [P, 8 * B])
        consts = sb("consts", [P, len(CONSTS), TPI])
        b_sb = sb("b_sb", [P, 1])
        Gh = sb("Gh", [P, H, P], F32R)
        Gl = sb("Gl", [P, H, P], F32R)
        Mh = sb("Mh", [P, H, P], F32R)
        Ml = sb("Ml", [P, H, P], F32R)
        bosT = sb("bosT", [P, B])
        wuT = sb("wuT", [P, FF], F32R)
        wdT = sb("wdT", [P, FT, P], F32R)
        xq = sb("xq", [P, NT, P])
        with ExitStack() as queries:
            xTh = queries.enter_context(nc.sbuf_tensor("xTh", [P, B * N], F32R))
        attnT = sb("attnT", [P, B * N])
        xTl = sb("xTl", [P, B * N], F32R)
        xT17 = sb("xT17", [P, ITERS, IBLK + 2, SEG])
        xw = [sb(f"xw{i}", [P, CPAIR, 3, P], F32R) for i in range(2)]

        with ExitStack() as prep:
            def pb(name, shape, dt=F32):
                return prep.enter_context(nc.sbuf_tensor(name, shape, dt))

            wT = pb("wT", [P, 24, P])
            PT = pb("PT", [P, H, P])
            wo_p = pb("wo_p", [P, 8, IL, H])
            w_sb = [pb(f"w_sb{i}", [P, INNER]) for i in range(3)]
            wo_sb = pb("wo_sb", [P, 8, P])
            R = pb("R", [P, H, P])
            w_ff = pb("w_ff", [P, 2, FF])
            tern = pb("tern", [P, 2, FF])
            xs = pb("xs", [P, NT, 2, P])
        with ExitStack() as attention:
            def ab(name, shape, dt=F32):
                return attention.enter_context(nc.sbuf_tensor(name, shape, dt))

            CTh, CTl = [], []
            for i in range(2):
                CTh.append(ab(f"CTh{i}", [P, H, CHUNK], F32R))
                CTl.append(ab(f"CTl{i}", [P, H, CHUNK], F32R))
            AT = [ab(f"AT{i}", [P, 2, 512], F32R) for i in range(2)]
            Yb = [ab(f"Yb{i}", [P, CHUNK // IL, P]) for i in range(2)]
            E = [ab(f"E{i}", [P, TILES, PITCH]) for i in range(2)]
            mx = [ab(f"mx{i}", [P, TILES]) for i in range(2)]
            sm = [ab(f"sm{i}", [P, TILES]) for i in range(2)]
            rc = [ab(f"rc{i}", [P, TILES]) for i in range(2)]
        attnS = sb("attnS", [P, ITER_TOK])
        res = sb("res", [P, TPI, P])
        x1 = sb("x1", [P, TPI, P])
        x1keep = sb("x1keep", [P, 2 * TPI, P])
        x1Th = sb("x1Th", [P, ITER_TOK], F32R)
        x1Tl = sb("x1Tl", [P, ITER_TOK], F32R)
        gS = [sb(f"gS{i}", [P, FF]) for i in range(2)]
        sq = sb("sq", [P, FF])
        dS = sb("dS", [P, ITER_TOK])
        y2 = sb("y2", [P, TPI, P])
        outS = sb("outS", [P, TPI, P])
        st = sb("st", [P, TPI, 6])
        mv = sb("mv", [P, TPI, 2])
        st2 = sb("st2", [P, TPI, 6])
        mv2 = sb("mv2", [P, TPI, 2])
        inv = sb("inv", [P, NT])
        hss = sb("hss", [P, TPI])
        hinv = sb("hinv", [P, TPI])
        rstd = sb("rstd", [P, TPI])
        rstd2 = sb("rstd2", [P, TPI])
        tiny = sb("tiny", [P, 8, TPI])
        hTh = sb("hTh", [P, FT, ITER_TOK], F32R)
        hTl = sb("hTl", [P, FT, ITER_TOK], F32R)

        bank = [ctx.enter_context(nc.psum_tensor(f"bank{i}", [P, 512], F32)) for i in range(8)]
        S_BANK, Y_BANK, T_BANK, C_BANK, O_BANK = [0, 1], [2, 3], 4, [5, 6], 7

        s_xq = [sem(f"s_xq{b}") for b in range(B)]
        s_wqkv = [sem(f"s_wqkv{c}") for c in range(3)]
        s_wout, s_small, s_wff = map(sem, ("s_wout", "s_small", "s_wff"))
        s_ident, s_pool, s_const, s_sel8, s_kron, s_zero = map(sem, (
            "s_ident", "s_pool", "s_const", "s_sel8", "s_kron", "s_zero"))
        s_fill, s_eva, s_evd = map(sem, ("s_fill", "s_evac_act", "s_evac_dve"))
        s_wop, s_xsh, s_xsl, s_xrows, s_pt, s_R = map(sem, ("s_wop", "s_xsh", "s_xsl", "s_xrows", "s_pt", "s_R"))
        s_asum, s_atot, s_thr, s_ternd, s_tern = map(sem, ("s_asum", "s_atot", "s_thr", "s_ternd", "s_tern"))
        s_mask, s_sel = sem("s_mask"), sem("s_sel")
        MASKS = 1 + 2 * 4 + 2
        s_win = [sem("s_win0"), sem("s_win1")]
        s_Y, s_Ye = sem("s_Y"), sem("s_Ye")
        s_S, s_max, s_sub, s_exp, s_sum, s_rec, s_norm = map(sem, (
            "s_S", "s_max", "s_sub", "s_exp", "s_sum", "s_rec", "s_norm"))
        s_T, s_ATh, s_ATl = map(sem, ("s_T", "s_ATh", "s_ATl"))
        s_C, s_CTh, s_CTl = map(sem, ("s_C", "s_CTh", "s_CTl"))
        s_O, s_Oe = sem("s_O"), sem("s_Oe")
        f_stage, f_aT, f_res, f_st, f_var, f_eps, f_rstd, f_x1, f_x1c, f_xT, f_xTh, f_xTl = map(sem, (
            "f_stage", "f_aT", "f_res", "f_st", "f_var", "f_eps", "f_rstd", "f_x1", "f_x1c", "f_xT", "f_xTh", "f_xTl"))
        f_rms, f_inv, f_hrms, f_hinv, f_eps2, f_rstd2 = map(sem, (
            "f_rms", "f_inv", "f_hrms", "f_hinv", "f_eps2", "f_rstd2"))
        f_up, f_gelu, f_sq, f_hT, f_hTh, f_hTl, f_dn, f_dnE, f_back = map(sem, (
            "f_up", "f_gelu", "f_sq", "f_hT", "f_hTh", "f_hTl", "f_dn", "f_dnE", "f_back"))
        f_y2, f_st2, f_var2, f_out, f_store, f_bosput, f_seen = map(sem, (
            "f_y2", "f_st2", "f_var2", "f_out", "f_store", "f_bosput", "f_seen"))
        f_seen_act = sem("f_seen_act")

        FILLS = ([("x", i, i, "AD") for i in range(4)]
                 + [("w", 4 + i, 4 + i, "A") for i in range(2)]
                 + [("p", i, (6, 7, 0, 1)[i], "AADD"[i]) for i in range(4)]
                 + [("w", i, (2, 3, 4, 5)[i], "ADAD"[i]) for i in range(4)]
                 + [("g", i, (6, 7, 0, 1)[i], "AD") for i in range(4)])
        TAIL = ([("v0", 0, T_BANK, "D"), ("t", 0, 5, "A"), ("t", 1, 6, "D"), ("bos", 0, O_BANK, "D")]
                + [("m", i, O_BANK, "AD") for i in range(4)])
        LAG = 2
        IN_STEP = [TAIL[0:4]] + [TAIL[4 + i:5 + i] for i in range(4)]
        ALLF = FILLS + TAIL

        def fill_no(kind, i):
            return next(n for n, f in enumerate(ALLF) if f[:2] == (kind, i)) + 1

        def read_no(who, kind, i):
            return sum(who in f[3] for f in ALLF[:fill_no(kind, i)])

        def bank_free(eng, kind, i):
            n = fill_no(kind, i) - 1
            for before in reversed(ALLF[:n]):
                if before[2] == ALLF[n][2]:
                    if "A" in before[3]:
                        eng.wait_ge(s_eva, read_no("A", *before[:2]))
                    if "D" in before[3]:
                        eng.wait_ge(s_evd, read_no("D", *before[:2]))
                    return

        WDMAS = 2 * 2 * (3 + 1)
        XROW_DMAS = 2 + 2 * (2 * ITERS + 2)

        AHEAD_SUB = AHEAD_O = AHEAD_OE = 2
        AHEAD_S = AHEAD_HINV = AHEAD_DNE = 1
        AHEAD_C, AHEAD_CT, AHEAD_ATL = 9, 2 * (LAG + 1), LAG + 1
        AHEAD_T = AHEAD_ATH = AHEAD_NORM = LAG
        AHEAD_GELU = AHEAD_HT = AHEAD_HTL = AHEAD_SQ = AHEAD_BACK = 2
        AHEAD_OUT = AHEAD_Y2 = TPI + 1
        AHEAD_HRMS = 3
        STORES = 3
        AHEAD_STORE = 16 * STORES

        def since(eng, I, j, d):
            return nullcontext() if j >= d else eng.If(I > 0)

        def before_last(eng, I, j):
            return nullcontext() if j < SLOTS // 2 else eng.If(I < ITERS - 1)

        def heads(i):
            return [8 * (i // 2) + i % 2 + 2 * k for k in range(4)]

        def Y_out(b, chunk_par, h0):
            return Yb[chunk_par][:, :, IL * h0:IL * h0 + 2 * IL].rearrange("p t (h i) -> p h t i", i=IL)

        def ct_view(buf, sc, q):
            v = buf[:, :, :].rearrange("p h (r q s) -> p h r q s", q=2, s=BLK)
            return v[:, :, 2 * sc:2 * sc + 2, q, :].rearrange("p h r s -> p r h s")

        def c_view(bk):
            return bank[C_BANK[bk]][:, :].rearrange("p (r h s) -> p r h s", r=2, s=BLK)

        def f32(ap):
            return ap.bitcast(F32)

        block = ctx.enter_context(nc.Block())

        @block.sync
        def _(sp):
            for b in range(B):
                t0 = b * (NT // B)
                sp.dma_start(xq[:, t0:t0 + 7, :], x[b, 1:897, :].rearrange("(m p) c -> p m c", p=P)).then_inc(s_xq[b], 16)
                sp.dma_start(xq[0:127, t0 + 7, :], x[b, 897:1024, :]).then_inc(s_xq[b], 16)
                sp.dma_start(xq[127:128, t0 + 7, :], x[b, 0:1, :]).then_inc(s_xq[b], 16)
            for c in (2, 0, 1):
                sp.dma_start(w_sb[c][:, :], w_qkv[:, c * INNER:(c + 1) * INNER]).then_inc(s_wqkv[c], 16)
                if c == 2:
                    sp.dma_start(wo_sb[:, :, :], w_out.rearrange("(t p) n -> p t n", p=P)).then_inc(s_wout, 16)
            for i in range(2):
                sp.dma_start(w_ff[:, i, :].rearrange("p (t d) -> p t d", t=FT) if i == 0 else w_ff[:, 1, :],
                             w_up.rearrange("(t p) d -> p t d", p=P) if i == 0 else w_down).then_inc(s_wff, 16)
            sp.dma_start(b_sb[:, :], b_out.rearrange("(c o) -> c o", o=1)).then_inc(s_small, 16)
            for k in range(IL):
                sp.dma_start(wth8[k:P:IL, :], w_th).then_inc(s_small, 16)
            sp.wait_ge(s_zero, 1)
            for it in (0, 2):
                sp.dma_start(x_rows[it, 0:LEAD, :], zrow[:, :]).then_inc(s_xrows, 16)
            sp.wait_ge(s_xsh, 1)
            sp.wait_ge(s_xsl, 1)
            for part in (slice(0, 2), slice(2, 3)):
                cols, n = slice(P * part.start, P * part.stop), part.stop - part.start
                for it in range(ITERS):
                    sp.dma_start(x_rows[it, LEAD:XROWS, cols].rearrange("(m p) c -> p m c", p=P),
                                 xs[:, TPI * it:TPI * it + TPI, 0:n, :].rearrange("p m s c -> p m (s c)")).then_inc(s_xrows, 16)
                    last = (it // 2 + 1) * (NT // B) - 1
                    sp.dma_start(bos_rows[it:it + 1, cols], xs[127:128, last, 0:n, :].rearrange("p s c -> p (s c)")).then_inc(s_xrows, 16)
                for it in (1, 3):
                    sp.dma_start(x_rows[it, 0:LEAD, cols],
                                 xs[P - LEAD:P, TPI * it - 1, 0:n, :].rearrange("p s c -> p (s c)")).then_inc(s_xrows, 16)
            sp.wait_ge(s_eva, read_no("A", "p", 3))
            sp.wait_ge(s_evd, read_no("D", "p", 3))
            sp.dma_start(pt_rows.rearrange("g o c -> o g c"), PT[:, :, :]).then_inc(s_pt, 16)
            sp.wait_ge(s_pt, 16)
            sp.dma_start(R[:, :, :], pt_rows.rearrange("g (a b) c -> (g a) b c", a=IL)).then_inc(s_R, 16)
            sp.wait_ge(s_xrows, 16 * XROW_DMAS)
            sp.wait_ge(s_zero, 4)
            with sp.Fori(0, ITERS) as I:
                for par in range(2):
                    sp.wait_ge(s_C, AHEAD_C + 16 * I - 8 + 8 * par)
                    for half in range(2):
                        for q in range(2):
                            first, n = ((0, 2) if half == 0 else (1, 2)) if q == half else (2 * q, 1)
                            cols = slice(P * first, P * (first + n))
                            for a in range(3):
                                m0, s0 = divmod(par * CHUNK + BLK * (q + a), 2 * BLK)
                                rows = x_rows.rearrange("i (m s) c -> i m s c", s=2 * BLK)
                                src = rows[I, m0:m0 + CPAIR, s0:s0 + BLK, cols].rearrange("m r c -> r m c")
                                row = 64 * half + SEG * a
                                sp.dma_start(f32(xw[par][row:row + BLK, :, first:first + n, :]).rearrange("p m s c -> p m (s c)"),
                                             src).then_inc(s_win[par], 16)
                            row = 64 * half + BLK
                            sp.dma_start(f32(xw[par][row:row + SEG + 1:SEG, :, first:first + n, :]).rearrange("p m s c -> p m (s c)"),
                                         bos_rows[I, cols].unsqueeze(0).unsqueeze(1).broadcast_to([2, CPAIR, n * P])).then_inc(s_win[par], 16)
            flat = out.rearrange("b n c -> (b n) c")
            sp.sem_inc(f_store, AHEAD_STORE)
            with sp.Fori(0, B) as b:
                for half in range(2):
                    sp.wait_ge(f_out, AHEAD_OUT + 8 * b + 4 * half + 4)
                    t = b * N + ITER_TOK * half
                    m = TPI - 1
                    sp.dma_start(flat[bass.ds(t + 1, m * P), :].rearrange("(m p) c -> p m c", p=P),
                                 outS[:, 0:m, :]).then_inc(f_store, 16)
                    sp.dma_start(flat[bass.ds(t + 1 + m * P, P - 1), :], outS[0:P - 1, m, :]).then_inc(f_store, 16)
                    sp.dma_start(flat[bass.ds(b * N + (ITER_TOK if half == 0 else 0), 1), :],
                                 outS[P - 1:P, TPI - 1, :]).then_inc(f_store, 16)
            sp.wait_ge(f_store, AHEAD_STORE + 16 * STORES * ITERS)

        @block.gpsimd
        def _(pool):
            nc.gpsimd.memset(ident[:, :], 0.0).then_inc(s_pool, 1)
            pool.wait_ge(s_pool, 1)
            nc.gpsimd.affine_select(out=ident[:, :], in_=ident[:, :], compare_op=ALU.not_equal, fill=1.0,
                                    base=0, pattern=[[-1, P]], channel_multiplier=1).then_inc(s_ident, 1)
            nc.gpsimd.memset(zrow[:, :], 0.0).then_inc(s_zero, 1)
            nc.gpsimd.memset(xT17[:, 0:3:2, 0:2, 0:BLK], 0.0).then_inc(s_zero, 1)
            nc.gpsimd.memset(sel[:, :], 0.0).then_inc(s_const, 1)
            m = mask[:, :, :].rearrange("p v (r f q w) -> p v r f q w", r=2, f=2, q=2)
            nc.gpsimd.memset(mask[:, :, :], 0.0).then_inc(s_mask, 1)
            pool.wait_ge(s_mask, 1)
            n = 1
            for v in range(2):
                for r in range(2):
                    for f in range(2):
                        own = m[0:IL, v, r, f, :, 2 * SEG:WIN]
                        nc.gpsimd.affine_select(out=own, in_=own, compare_op=ALU.is_ge, fill=NEG, base=IL * f,
                                                pattern=[[0, 2], [-1, BLK]], channel_multiplier=1).then_inc(s_mask, 1)
                        n += 1
                        nc.gpsimd.memset(m[0:IL, v, r, f, :, 2 * SEG - 1:2 * SEG], NEG)
            for f in range(2):
                nc.gpsimd.memset(m[0:IL, 0, 0, f, :, 0:BLK], NEG)
                nc.gpsimd.memset(m[0:IL, 0, 0, f, 0, SEG:SEG + BLK], NEG).then_inc(s_mask, 1)
            for i in range(2):
                nc.gpsimd.memset(E[i][:, :, :], 0.0)
            for c, value in enumerate(CONSTS):
                nc.gpsimd.memset(consts[:, c, :], value)
            pool.wait_ge(s_xsh, 1)
            nc.gpsimd.tensor_tensor(xs[:, :, 1, :], xq[:, :, :], xs[:, :, 0, :], ALU.subtract).then_inc(s_xsl, 1)
            for i in range(2):
                nc.gpsimd.memset(f32(xw[i][:, :, :, :]), 0.0).then_inc(s_zero, 1)
            pool.wait_ge(s_asum, 2)
            nc.gpsimd.partition_all_reduce(tsum[:, 2:4], tsum[:, 0:2], P, RADD).then_inc(s_atot, 1)

            pool.sem_inc(s_norm, AHEAD_NORM)
            with pool.Fori(0, ITERS) as I:
                for j in range(SLOTS):
                    e = E[j % 2][:, :, 0:WIN]
                    pool.wait_ge(s_rec, SLOTS * I + j + 1)
                    nc.gpsimd.tensor_tensor(e, e, rc[j % 2][:, :].unsqueeze(2).broadcast_to([P, TILES, WIN]),
                                            ALU.mult).then_inc(s_norm, 1)

            tt = nc.gpsimd.tensor_tensor

            pool.sem_inc(f_hrms, AHEAD_HRMS)
            pool.sem_inc(f_hinv, AHEAD_HINV)
            def scale(g):
                pool.wait_ge(f_var, 4 * g + 4)
                tt(tiny[:, 0, :], mv[:, :, 1], consts[:, C_EPS_LN, :], ALU.add).then_inc(f_eps, 1)
                pool.wait_ge(f_eps, g + 1)
                tt(rstd[:, :], tiny[:, 0, :], consts[:, MINUS_HALF, :], ALU.pow).then_inc(f_rstd, 1)

            def up_scale(g):
                tt(tiny[:, 1, :], mv[:, :, 1], consts[:, HALF, :], ALU.pow).then_inc(f_rms, 1)
                pool.wait_ge(f_rms, 3 * g + 1)
                pool.wait_ge(f_rstd, g + 1)
                tt(tiny[:, 2, :], tiny[:, 1, :], rstd[:, :], ALU.mult).then_inc(f_rms, 1)
                pool.wait_ge(f_rms, 3 * g + 2)
                tt(tiny[:, 3, :], tiny[:, 2, :], consts[:, C_EPS_RMS, :], ALU.add).then_inc(f_rms, 1)
                pool.wait_ge(f_rms, 3 * g + 3)
                tt(inv[:, bass.ds(g % ITERS * TPI, TPI)], tiny[:, 3, :], consts[:, MINUS_ONE, :], ALU.pow).then_inc(f_inv, 1)

            def down_scale(g):
                pool.wait_ge(f_sq, AHEAD_SQ + 4 * g)
                tt(tiny[:, 4, :], hss[:, :], consts[:, C_PER_FF, :], ALU.mult).then_inc(f_hrms, 1)
                pool.wait_ge(f_hrms, AHEAD_HRMS + 3 * g - 2)
                tt(tiny[:, 5, :], tiny[:, 4, :], consts[:, HALF, :], ALU.pow).then_inc(f_hrms, 1)
                pool.wait_ge(f_hrms, AHEAD_HRMS + 3 * g - 1)
                tt(tiny[:, 6, :], tiny[:, 5, :], consts[:, C_EPS_RMS, :], ALU.add).then_inc(f_hrms, 1)
                pool.wait_ge(f_hrms, AHEAD_HRMS + 3 * g)
                pool.wait_ge(f_y2, AHEAD_Y2 + 4 * g - 4)
                tt(hinv[:, :], tiny[:, 6, :], consts[:, MINUS_ONE, :], ALU.pow).then_inc(f_hinv, 1)

            def scale2(g):
                pool.wait_ge(f_var2, 4 * g)
                tt(tiny[:, 7, :], mv2[:, :, 1], consts[:, C_EPS_LN, :], ALU.add).then_inc(f_eps2, 1)
                pool.wait_ge(f_eps2, g)
                tt(rstd2[:, :], tiny[:, 7, :], consts[:, MINUS_HALF, :], ALU.pow).then_inc(f_rstd2, 1)

            scale(0)
            up_scale(0)
            with pool.Fori(0, ITERS + 1) as g:
                with pool.If(g > 0):
                    down_scale(g)
                with pool.If(g < ITERS - 1):
                    scale(g + 1)
                    up_scale(g + 1)
                with pool.If(g > 0):
                    scale2(g)

        @block.scalar
        def _(act):
            copy = lambda o, i, **k: nc.scalar.activation(o, i, ACT.Copy, **k)
            def fills(fs):
                for kind, i, bk, who in fs:
                    if "A" not in who:
                        continue
                    act.wait_ge(s_fill, fill_no(kind, i))
                    if kind == "x":
                        copy(xTh[:, 512 * i:512 * (i + 1)], bank[bk][:, :]).then_inc(s_eva, 1)
                        if i == 3:
                            copy(xs[:, :, 0, :].bitcast(F32R), xq[:, :, :]).then_inc(s_xsh, 1)
                    elif kind == "w":
                        if i == 4:
                            act.wait_ge(s_wout, 16)
                            copy(wo_p[:, :, :, :], wo_sb[:, :, :].rearrange("p t (b a) -> p t a b", a=IL)).then_inc(s_wop, 1)
                        copy(wT[:, 4 * i:4 * i + 4, :], bank[bk][:, :].rearrange("p (t c) -> p t c", t=4)).then_inc(s_eva, 1)
                    elif kind == "g":
                        hs = heads(i)
                        copy(Gh[:, hs[0]:hs[-1] + 1:2, :], bank[bk][:, :].rearrange("p (t c) -> p t c", t=4),
                             scale=SCALE).then_inc(s_eva, 1)
                    elif kind == "p":
                        hs = heads(i)
                        copy(PT[:, hs[0]:hs[-1] + 1:2, :], bank[bk][:, :].rearrange("p (t c) -> p t c", t=4)).then_inc(s_eva, 1)
                    elif kind == "m":
                        o = Mh[:, :, 32 * i:32 * i + 32].rearrange("p h (a b) -> p a h b", b=IL)
                        copy(o, bank[bk][:, :].rearrange("p (a h b) -> p a h b", a=4, b=IL)).then_inc(s_eva, 1)
                    elif kind == "t":
                        copy(wuT[:, :], bank[bk][:, :]).then_inc(s_eva, 1)

            fills(FILLS)
            for b in range(8):
                act.wait_ge(s_Y, b + 1)
                copy(Y_out(b, 0, 2 * b), bank[Y_BANK[b % 2]][:, :].rearrange("p (h t i) -> p h t i", h=2, i=IL)).then_inc(s_Ye, 1)
            act.wait_ge(s_xrows, 16 * XROW_DMAS)

            def ct_hi(j, t2):
                sc, par = (j - LAG - 1) % 4, ((j - LAG - 1) // 4) % 2
                for bk in range(2):
                    act.wait_ge(s_C, AHEAD_C + t2 + 1 + bk)
                    copy(ct_view(CTh[par], sc, bk), c_view(bk)).then_inc(s_CTh, 1)

            def at_hi(j, t):
                act.wait_ge(s_T, AHEAD_T + t)
                for q in range(2):
                    half = slice(64 * q, 64 * q + 64)
                    ins = copy(AT[(j - LAG) % 2][half, q, :], bank[T_BANK][half, :])
                ins.then_inc(s_ATh, 1)

            act.sem_inc(s_CTh, AHEAD_CT)
            act.sem_inc(s_ATh, AHEAD_ATH)
            act.sem_inc(s_Oe, AHEAD_OE)
            with act.Fori(0, ITERS) as I:
                for j in range(SLOTS):
                    if j == 1 + LAG:
                        act.wait_ge(s_O, AHEAD_O + 2 * I - 1)
                    if j == 5 + LAG:
                        act.wait_ge(s_O, AHEAD_O + 2 * I)
                    with since(act, I, j, LAG + 1):
                        ct_hi(j, 16 * I + 2 * (j - LAG - 1))
                    with since(act, I, j, LAG):
                        at_hi(j, SLOTS * I + j + 1 - LAG)

                    def y_out(b):
                        with before_last(act, I, j):
                            if j % 4 == 0 and b == 0:
                                act.wait_ge(s_S, AHEAD_S + SLOTS * I + j)
                            act.wait_ge(s_Y, 16 * I + 2 * j + b + 9)
                            copy(Y_out(b, (j // 4 + 1) % 2, 4 * (j % 4) + 2 * b),
                                 bank[Y_BANK[b]][:, :].rearrange("p (h t i) -> p h t i", h=2, i=IL)).then_inc(s_Ye, 1)
                    y_out(0)
                    e = E[j % 2][:, :, 0:WIN]
                    act.wait_ge(s_sub, AHEAD_SUB + SLOTS * I + j + 1)
                    nc.scalar.activation(e, e, ACT.Exp).then_inc(s_exp, 1)
                    y_out(1)
                    if j < len(IN_STEP):
                        with act.If(I < 1):
                            fills(IN_STEP[j])
                    if j % 4 == LAG - 1:
                        with act.If(I > 0):
                            act.wait_ge(s_O, AHEAD_O + 2 * I - 1 + j // 4)
                            copy(attnT[:, bass.ds((2 * I + 2 * ITERS - 2 + j // 4) % (2 * ITERS) * CHUNK, CHUNK)],
                                 bank[O_BANK][:, 0:CHUNK]).then_inc(s_Oe, 1)
            last = SLOTS * ITERS
            for j in range(LAG):
                ct_hi(j, 2 * (last + j - LAG - 1))
                at_hi(j, last + j + 1 - LAG)
            act.wait_ge(s_O, AHEAD_O + 2 * ITERS - 1)
            copy(attnT[:, (2 * ITERS - 2) * CHUNK:(2 * ITERS - 1) * CHUNK], bank[O_BANK][:, 0:CHUNK]).then_inc(s_Oe, 1)
            ct_hi(LAG, 2 * last - 2)

            def x1_hi(g, first=False):
                if not first:
                    act.wait_ge(f_up, 4 * g)
                act.wait_ge(f_xT, g + 1)
                copy(x1Th[:, :], bank[1][:, :]).then_inc(f_xTh, 1)

            def gelu(g, i):
                act.wait_ge(f_up, 4 * g + i + 1)
                act.wait_ge(f_hT, AHEAD_HT + 4 * g + i - 1)
                act.wait_ge(f_sq, AHEAD_SQ + 4 * g + i - 1)
                act.sem_inc(f_seen_act, 1)
                nc.scalar.activation(gS[i % 2][:, :], bank[2 + i % 2][:, :], ACT.Gelu,
                                     scale=inv[:, bass.ds(g * TPI + i, 1)]).then_inc(f_gelu, 1)

            def squares(g, i):
                act.wait_ge(f_gelu, AHEAD_GELU + 4 * g + i + 1)
                act.wait_ge(f_sq, AHEAD_SQ + 4 * g + i)
                nc.scalar.activation(sq[:, :], gS[i % 2][:, :], ACT.Square, accum_out=hss[:, i:i + 1]).then_inc(f_sq, 1)

            def h_hi(g, i):
                act.wait_ge(f_hT, AHEAD_HT + 4 * g + i + 1)
                copy(hTh[:, :, P * i:P * i + P], bank[4 + i % 2][:, :].rearrange("p (t c) -> p t c", t=FT)).then_inc(f_hTh, 1)

            def down_out(g):
                act.wait_ge(f_dn, g)
                act.wait_ge(f_back, AHEAD_BACK + g - 1)
                copy(dS[:, :], bank[6][:, :]).then_inc(f_dnE, 1)

            act.sem_inc(f_gelu, AHEAD_GELU)
            act.sem_inc(f_sq, AHEAD_SQ)
            act.sem_inc(f_dnE, AHEAD_DNE)
            x1_hi(0, first=True)
            act.wait_ge(s_O, AHEAD_O + 2 * ITERS)
            copy(attnT[:, (2 * ITERS - 1) * CHUNK:2 * ITERS * CHUNK], bank[O_BANK][:, 0:CHUNK]).then_inc(s_Oe, 1)
            with act.Fori(0, ITERS) as g:
                act.wait_ge(f_inv, g + 1)
                act.sem_inc(f_seen_act, 1)
                gelu(g, 0)
                gelu(g, 1)
                act.wait_ge(f_hinv, AHEAD_HINV + g)
                squares(g, 0)
                with act.If(g > 0):
                    down_out(g)
                act.wait_ge(f_dn, g)
                h_hi(g, 0)
                gelu(g, 2)
                squares(g, 1)
                h_hi(g, 1)
                gelu(g, 3)
                squares(g, 2)
                h_hi(g, 2)
                with act.If(g < ITERS - 1):
                    x1_hi(g + 1)
                squares(g, 3)
                h_hi(g, 3)
            down_out(ITERS)

        @block.vector
        def _(dve):
            v = nc.vector
            dve.wait_ge(s_ident, 1)
            v.tensor_reduce(sel8[:, :], ident[:, :].rearrange("p (g k) -> p k g", k=IL), AX.X, ALU.add).then_inc(s_sel8, 1)
            def fills(fs):
                for kind, i, bk, who in fs:
                    if "D" not in who:
                        continue
                    dve.wait_ge(s_fill, fill_no(kind, i))
                    if kind == "x":
                        dve.wait_ge(s_eva, read_no("A", kind, i))
                        v.tensor_copy(xT17[:, i, 2:IBLK + 2, 0:BLK], bank[bk][:, :].rearrange("p (u s) -> p u s", s=BLK))
                        if i % 2 == 0:
                            v.tensor_copy(xT17[:, i + 1, 0:2, 0:BLK],
                                          bank[bk][:, 512 - LEAD:512].rearrange("p (u s) -> p u s", s=BLK))
                        else:
                            v.tensor_copy(xT17[:, i - 1:i + 1, :, BLK],
                                          bank[bk][:, 511:512].unsqueeze(2).broadcast_to([P, 2, IBLK + 2]))
                        o = slice(512 * i, 512 * (i + 1))
                        v.tensor_tensor(xTl[:, o], bank[bk][:, :], f32(xTh[:, o]), ALU.subtract).then_inc(s_evd, 1)
                    elif kind == "w":
                        v.tensor_copy(wT[:, 4 * i:4 * i + 4, :], bank[bk][:, :].rearrange("p (t c) -> p t c", t=4)).then_inc(s_evd, 1)
                    elif kind == "g":
                        hs = heads(i)
                        o = slice(hs[0], hs[-1] + 1, 2)
                        dve.wait_ge(s_eva, read_no("A", kind, i))
                        v.scalar_tensor_tensor(out=Gl[:, o, :], in0=bank[bk][:, :].rearrange("p (t c) -> p t c", t=4),
                                               scalar=SCALE, in1=f32(Gh[:, o, :]), op0=ALU.mult,
                                               op1=ALU.subtract).then_inc(s_evd, 1)
                    elif kind == "p":
                        hs = heads(i)
                        v.tensor_copy(PT[:, hs[0]:hs[-1] + 1:2, :], bank[bk][:, :].rearrange("p (t c) -> p t c", t=4)).then_inc(s_evd, 1)
                    elif kind == "m":
                        o = slice(32 * i, 32 * i + 32)
                        dve.wait_ge(s_eva, read_no("A", kind, i))
                        v.tensor_tensor(Ml[:, :, o].rearrange("p h (a b) -> p a h b", b=IL),
                                        bank[bk][:, :].rearrange("p (a h b) -> p a h b", a=4, b=IL),
                                        f32(Mh[:, :, o]).rearrange("p h (a b) -> p a h b", b=IL),
                                        ALU.subtract).then_inc(s_evd, 1)
                    elif kind == "t":
                        v.tensor_copy(wdT[:, :, :], bank[bk][:, :].rearrange("p (t c) -> p t c", t=4)).then_inc(s_evd, 1)
                    elif kind == "v0":
                        v.tensor_copy(v0T[:, :], bank[bk][:, 0:16]).then_inc(s_evd, 1)
                    elif kind == "bos":
                        v.tensor_copy(bosT[:, :], bank[bk][:, 0:B]).then_inc(s_evd, 1)

            fills(FILLS)
            dve.wait_ge(s_const, 1)
            v.tensor_copy(sel[0:IL, :].rearrange("p (h k) -> p h k", k=IL),
                          ident[0:IL, 0:IL].unsqueeze(1).broadcast_to([IL, H, IL])).then_inc(s_sel, 1)
            dve.wait_ge(s_small, 16 * (IL + 1))
            dve.wait_ge(s_sel8, 1)
            v.tensor_tensor(kron[:, :].rearrange("p (h k) -> p h k", k=IL),
                            wth8[:, :].unsqueeze(2).broadcast_to([P, H, IL]),
                            sel8[:, :].unsqueeze(1).broadcast_to([P, H, IL]), ALU.mult).then_inc(s_kron, 1)
            dve.wait_ge(s_wff, 32)
            for k in range(2):
                v.tensor_reduce(tsum[:, k:k + 1], w_ff[:, k, :], AX.X, ALU.add, apply_absolute_value=True).then_inc(s_asum, 1)
            dve.wait_ge(s_atot, 1)
            v.tensor_scalar(tsum[:, 4:6], tsum[:, 2:4], 1.0 / (FF * D), 0.5, ALU.mult, ALU.mult).then_inc(s_thr, 1)
            v.tensor_scalar(tsum[:, 6:8], tsum[:, 2:4], 1.0 / (FF * D), -0.5, ALU.mult, ALU.mult).then_inc(s_thr, 1)
            dve.wait_ge(s_thr, 2)
            for k in range(2):
                v.tensor_scalar(tern[:, k, :], w_ff[:, k, :], tsum[:, 6 + k:7 + k], None, ALU.is_lt).then_inc(s_ternd, 1)
            dve.wait_ge(s_ternd, 2)
            for k in range(2):
                v.scalar_tensor_tensor(out=w_ff[:, k, :], in0=w_ff[:, k, :], scalar=tsum[:, 4 + k:5 + k],
                                       in1=tern[:, k, :], op0=ALU.is_gt, op1=ALU.subtract).then_inc(s_tern, 1)

            def ct_lo(j, t2):
                sc, par = (j - LAG - 1) % 4, ((j - LAG - 1) // 4) % 2
                for bk in range(2):
                    dve.wait_ge(s_CTh, AHEAD_CT + t2 + 1 + bk)
                    v.tensor_tensor(ct_view(CTl[par], sc, bk), c_view(bk), ct_view(f32(CTh[par][:, :, :]), sc, bk),
                                    ALU.subtract).then_inc(s_CTl, 1)

            def at_lo(j, t):
                dve.wait_ge(s_ATh, AHEAD_ATH + t)
                for q in range(2):
                    half, other = slice(64 * q, 64 * q + 64), slice(64 - 64 * q, 128 - 64 * q)
                    ins = v.tensor_tensor(AT[(j - LAG) % 2][other, q, :], bank[T_BANK][half, :],
                                          f32(AT[(j - LAG) % 2][half, q, :]), ALU.subtract)
                ins.then_inc(s_ATl, 1)

            dve.sem_inc(s_CTl, AHEAD_CT)
            dve.sem_inc(s_sub, AHEAD_SUB)
            dve.sem_inc(s_ATl, AHEAD_ATL)
            with dve.Fori(0, ITERS) as I:
                for j in range(SLOTS):
                    k = j % 2
                    with since(dve, I, j, LAG + 1):
                        ct_lo(j, 16 * I + 2 * (j - LAG - 1))
                    with since(dve, I, j, LAG):
                        at_lo(j, SLOTS * I + j + 1 - LAG)
                    s = bank[S_BANK[k]][:, 0:TILES * WIN].rearrange("p (t w) -> p t w", w=WIN)
                    e = E[k][:, :, 0:WIN]
                    dve.wait_ge(s_S, AHEAD_S + SLOTS * I + j + 1)
                    v.tensor_reduce(mx[k][:, :], s, AX.X, ALU.max).then_inc(s_max, 1)
                    dve.wait_ge(s_max, SLOTS * I + j + 1)
                    v.tensor_tensor(e, s, mx[k][:, :].unsqueeze(2).broadcast_to([P, TILES, WIN]),
                                    ALU.subtract).then_inc(s_sub, 1)
                    dve.wait_ge(s_exp, SLOTS * I + j + 1)
                    v.tensor_reduce(sm[k][:, :], e, AX.X, ALU.add).then_inc(s_sum, 1)
                    dve.wait_ge(s_sum, SLOTS * I + j + 1)
                    v.reciprocal(rc[k][:, :], sm[k][:, :]).then_inc(s_rec, 1)
                    if j < len(IN_STEP):
                        with dve.If(I < 1):
                            fills(IN_STEP[j])
            last = SLOTS * ITERS
            for j in range(LAG):
                ct_lo(j, 2 * (last + j - LAG - 1))
                at_lo(j, last + j + 1 - LAG)

            def bos_row(b, chunks):
                dve.wait_ge(s_Oe, AHEAD_OE + chunks)
                v.tensor_copy(attnT[:, b * N + N - 1:b * N + N], bosT[:, b:b + 1]).then_inc(f_bosput, 1)
                dve.wait_ge(f_bosput, b + 1)

            def stage(g):
                dve.wait_ge(f_aT, g)
                v.tensor_scalar(attnS[:, :], attnT[:, bass.ds(g % ITERS * ITER_TOK, ITER_TOK)], b_sb[:, 0:1], None,
                                ALU.add).then_inc(f_stage, 1)

            def residual(g):
                dve.wait_ge(f_aT, g + 1)
                v.tensor_tensor(res[:, :, :], bank[0][:, :].rearrange("p (t c) -> p t c", t=TPI),
                                xq[:, bass.ds(g % ITERS * TPI, TPI), :], ALU.add).then_inc(f_res, 1)
                dve.wait_ge(f_res, g + 1)
                for i in range(TPI):
                    v.bn_stats(st[:, i, :], res[:, i, :]).then_inc(f_st, 1)
                dve.wait_ge(f_inv, g)
                dve.wait_ge(f_st, 4 * g + 4)
                dve.sem_inc(f_seen, 1)
                for i in range(TPI):
                    v.bn_aggr(mv[:, i, :], st[:, i, :]).then_inc(f_var, 1)

            def layernorm(g):
                dve.wait_ge(f_xT, g)
                dve.wait_ge(f_x1c, g)
                dve.wait_ge(f_rstd, g + 1)
                for i in range(TPI):
                    v.tensor_scalar(x1[:, i, :], res[:, i, :], mv[:, i, 0:1], rstd[:, i:i + 1], ALU.subtract,
                                    ALU.mult).then_inc(f_x1, 1)

            def x1_lo(g):
                dve.wait_ge(f_xTh, g + 1)
                v.tensor_tensor(x1Tl[:, :], bank[1][:, :], f32(x1Th[:, :]), ALU.subtract).then_inc(f_xTl, 1)

            def h_lo(g, i):
                dve.wait_ge(f_hTh, 4 * g + i + 1)
                c = slice(P * i, P * i + P)
                v.tensor_tensor(hTl[:, :, c], bank[4 + i % 2][:, :].rearrange("p (t c) -> p t c", t=FT),
                                f32(hTh[:, :, c]), ALU.subtract).then_inc(f_hTl, 1)

            def keep(g):
                dve.wait_ge(f_y2, AHEAD_Y2 + 4 * g - 4)
                dve.sem_inc(f_seen, 1)
                dve.wait_ge(f_x1, 4 * g + 4)
                v.tensor_copy(x1keep[:, bass.ds(g % 2 * TPI, TPI), :], x1[:, :, :]).then_inc(f_x1c, 1)

            def second(g):
                dve.wait_ge(f_back, AHEAD_BACK + g)
                dve.wait_ge(f_hinv, AHEAD_HINV + g)
                dve.wait_ge(f_x1c, g)
                dve.wait_ge(f_out, AHEAD_OUT + 4 * g - 4)
                for i in range(TPI):
                    v.scalar_tensor_tensor(out=y2[:, i:i + 1, :], in0=bank[7][:, P * i:P * i + P].unsqueeze(1),
                                           scalar=hinv[:, i:i + 1], in1=x1keep[:, bass.ds((g + 1) % 2 * TPI + i, 1), :],
                                           op0=ALU.mult, op1=ALU.add).then_inc(f_y2, 1)
                for i in range(TPI):
                    dve.wait_ge(f_y2, AHEAD_Y2 + 4 * g - 3 + i)
                    v.bn_stats(st2[:, i, :], y2[:, i, :]).then_inc(f_st2, 1)
                dve.wait_ge(f_st2, 4 * g)
                dve.sem_inc(f_seen, 1)
                for i in range(TPI):
                    v.bn_aggr(mv2[:, i, :], st2[:, i, :]).then_inc(f_var2, 1)

            def result(g):
                dve.wait_ge(f_store, AHEAD_STORE + 16 * STORES * (g - 1))
                dve.sem_inc(f_seen, 1)
                dve.wait_ge(f_rstd2, g)
                for i in range(TPI):
                    v.tensor_scalar(outS[:, i, :], y2[:, i, :], mv2[:, i, 0:1], rstd2[:, i:i + 1], ALU.subtract,
                                    ALU.mult).then_inc(f_out, 1)

            dve.sem_inc(f_hTl, AHEAD_HTL)
            dve.sem_inc(f_y2, AHEAD_Y2)
            dve.sem_inc(f_out, AHEAD_OUT)
            bos_row(0, 2 * ITERS - 1)
            stage(0)
            ct_lo(LAG, 2 * last - 2)
            residual(0)
            layernorm(0)
            stage(1)
            x1_lo(0)
            bos_row(1, 2 * ITERS)
            with dve.Fori(0, ITERS) as g:
                keep(g)
                with dve.If(g < ITERS - 1):
                    residual(g + 1)
                with dve.If(g < ITERS - 2):
                    stage(g + 2)
                h_lo(g, 0)
                with dve.If(g < ITERS - 1):
                    layernorm(g + 1)
                h_lo(g, 1)
                with dve.If(g > 0):
                    second(g)
                with dve.If(g < ITERS - 1):
                    x1_lo(g + 1)
                h_lo(g, 2)
                h_lo(g, 3)
                with dve.If(g > 0):
                    result(g)
            second(ITERS)
            result(ITERS)

        @block.tensor
        def _(pe):
            mm = nc.tensor.matmul

            def split3(o, wh, wl, rh, rl, start=True, stop=True, **k):
                mm(o, wh, rh, start=start, stop=False, **k)
                mm(o, wh, rl, start=False, stop=False, **k)
                return mm(o, wl, rh, start=False, stop=stop, **k)

            def y_part(bk, chunk_cols, h0):
                for n in range(2):
                    ins = split3(bank[Y_BANK[bk]][:, CHUNK * n:CHUNK * (n + 1)], Gh[:, h0 + n, :], Gl[:, h0 + n, :],
                                 xTh[:, chunk_cols], xTl[:, chunk_cols])
                ins.then_inc(s_Y, 1)

            def fills(fs):
                for kind, i, bk, who in fs:
                    bank_free(pe, kind, i)
                    bnk = bank[bk]
                    if kind == "x":
                        if i % 2 == 0:
                            pe.wait_ge(s_ident, 1)
                            pe.wait_ge(s_xq[i // 2], 48)
                        for k in range(4):
                            ins = nc.tensor.transpose(bnk[:, P * k:P * k + P], xq[:, 4 * i + k, :], ident[:, :])
                    elif kind == "w":
                        pe.wait_ge(s_wqkv[i // 2], 16)
                        for k in range(4):
                            c = P * (4 * (i % 2) + k)
                            ins = nc.tensor.transpose(bnk[:, P * k:P * k + P], w_sb[i // 2][:, c:c + P], ident[:, :])
                    elif kind == "g":
                        if i == 0:
                            for n in (2, 3):
                                pe.wait_ge(s_eva if n % 2 == 0 else s_evd, read_no("AD"[n % 2], "w", n))
                        for k, h in enumerate(heads(i)):
                            r = slice(DH * (h % 2), DH * (h % 2) + DH)
                            ins = mm(bnk[:, P * k:P * k + P], wT[r, h // 2, :], wT[r, 8 + h // 2, :], start=True, stop=True)
                    elif kind == "p":
                        if i == 0:
                            pe.wait_ge(s_wop, 1)
                            pe.wait_ge(s_eva, read_no("A", "w", 5))
                        for k, h in enumerate(heads(i)):
                            r = slice(DH * (h % 2), DH * (h % 2) + DH)
                            o = wo_p[r, h // 2, :, :].rearrange("p a b -> p (a b)")
                            ins = mm(bnk[:, P * k:P * k + P], o, wT[r, 16 + h // 2, :], start=True, stop=True)
                    elif kind == "m":
                        if i == 0:
                            pe.wait_ge(s_R, 16)
                            pe.wait_ge(s_kron, 1)
                        for k in range(4):
                            ins = mm(bnk[:, P * k:P * k + P], R[:, 4 * i + k, :], kron[:, :], start=True, stop=True)
                    elif kind == "t":
                        pe.wait_ge(s_tern, 2)
                        for k in range(4):
                            ins = nc.tensor.transpose(bnk[:, P * k:P * k + P], w_ff[:, i, P * k:P * k + P], ident[:, :])
                    elif kind == "v0":
                        for k in range(8):
                            c = P * k
                            ins = mm(bnk[:, 2 * k:2 * k + 2], w_sb[2][:, c:c + P], xT17[:, 0:3:2, 0, BLK], start=True, stop=True)
                    elif kind == "bos":
                        pe.wait_ge(s_evd, read_no("D", "v0", 0))
                        for k in range(8):
                            ins = mm(bnk[:, 0:2], wo_sb[:, k, :], v0T[:, 2 * k:2 * k + 2], start=(k == 0), stop=(k == 7))
                    ins.then_inc(s_fill, 1)

            fills(FILLS)
            for b in range(8):
                if b % 4 == 0:
                    pe.wait_ge(s_eva, read_no("A", "g", 1 + b // 2))
                    pe.wait_ge(s_evd, read_no("D", "g", 1 + b // 2))
                if b >= 2:
                    pe.wait_ge(s_Ye, b - 1)
                y_part(b % 2, slice(0, CHUNK), 2 * b)
            pe.wait_ge(s_zero, 4)
            pe.wait_ge(s_mask, MASKS)
            pe.wait_ge(s_sel, 1)

            def transposes(j, t):
                pe.wait_ge(s_norm, AHEAD_NORM + t)
                for r in range(2):
                    for f in range(2):
                        o = bank[T_BANK][:, 256 * r:256 * r + 256].rearrange("p (h s) -> p h s", s=BLK)
                        k = 4 * r + 2 * f
                        ins = nc.tensor.transpose(o[:, :, IL * f:IL * f + IL],
                                                  E[(j - LAG) % 2][:, k:k + 2, :].rearrange("p t w -> p (t w)"), ident[:, :])
                ins.then_inc(s_T, 1)

            def c_part(j):
                sc, par, k = (j - LAG) % 4, ((j - LAG) // 4) % 2, (j - LAG) % 2
                for r in range(2):
                    ins = []
                    for q in range(2):
                        row, col = slice(64 * q, 64 * q + WIN), slice(256 * r, 256 * r + 256)
                        m, both = 2 * sc + r, slice(0, 64 + WIN)
                        mm(bank[C_BANK[q]][:, col], xw[par][both, m, 2 * q, :], AT[k][both, q, col], start=True, stop=False)
                        ins.append(mm(bank[C_BANK[q]][:, col], xw[par][row, m, 1, :], AT[k][row, q, col],
                                      start=False, stop=True))
                for i in ins:
                    i.then_inc(s_C, 1)

            def o_part(p, par):
                for h in range(4 * p, 4 * p + 4):
                    ins = split3(bank[O_BANK][:, 0:CHUNK], Mh[:, h, :], Ml[:, h, :], CTh[par][:, h, :], CTl[par][:, h, :],
                                 start=(h == 0), stop=(h == H - 1))
                if p == 3:
                    ins.then_inc(s_O, 1)

            pe.sem_inc(s_C, AHEAD_C)
            pe.sem_inc(s_S, AHEAD_S)
            pe.sem_inc(s_T, AHEAD_T)
            pe.sem_inc(s_O, AHEAD_O)
            with pe.Fori(0, ITERS) as I:
                for j in range(SLOTS):
                    k = j % 2
                    with since(pe, I, j, LAG):
                        pe.wait_ge(s_ATl, AHEAD_ATL + SLOTS * I + j - LAG)
                        transposes(j, SLOTS * I + j + 1 - LAG)
                    pe.wait_ge(s_sub, AHEAD_SUB + SLOTS * I + j - 1)
                    if j % 4 == 0:
                        pe.wait_ge(s_Ye, 16 * I + 2 * j + 8)
                    for tile in range(TILES):
                        r, f, q = tile // 4, tile // 2 % 2, tile % 2
                        blk = STEP_BLK * j + 2 * r + q
                        ytile = 2 * (blk % CBLK) + f
                        keys = xT17[:, bass.ds(I, 1), :, :].rearrange("p i u s -> p (i u s)")[:, SEG * blk:SEG * blk + WIN]
                        mm(bank[S_BANK[k]][:, WIN * tile:WIN * tile + WIN], Yb[(j // 4) % 2][:, ytile, :], keys,
                           start=(tile == 0), stop=False, skip_group_check=True)
                    if j == 0:
                        ins = mm(bank[S_BANK[k]][:, 0:TILES * WIN], sel[:, :],
                                 mask[:, bass.ds(I % 2, 1), :].rearrange("p a w -> p (a w)"),
                                 start=False, stop=True, skip_group_check=True)
                    else:
                        late = slice(2 * SEG - 1, WIN)
                        ins = mm(bank[S_BANK[k]][:, 0:TILES * WIN].rearrange("p (t w) -> p t w", w=WIN)[:, :, late], sel[:, :],
                                 mask[:, 1, :].rearrange("p (t w) -> p t w", w=WIN)[:, :, late],
                                 start=False, stop=True, skip_group_check=True)
                    ins.then_inc(s_S, 1)
                    with before_last(pe, I, j):
                        for b in range(2):
                            pe.wait_ge(s_Ye, 16 * I + 2 * j + b + 7)
                            y_part(b, bass.ds((2 * I + j // 4 + 1) % (2 * ITERS) * CHUNK, CHUNK), 4 * (j % 4) + 2 * b)
                    if j < len(IN_STEP):
                        with pe.If(I < 1):
                            fills(IN_STEP[j])
                    if j == LAG:
                        pe.wait_ge(s_eva, read_no("A", "t", 0))
                        pe.wait_ge(s_evd, read_no("D", "t", 1))
                    if j == 4 + LAG:
                        pe.wait_ge(s_eva, read_no("A", "m", 3))
                        pe.wait_ge(s_evd, read_no("D", "m", 3))
                    with since(pe, I, j, 4 + LAG):
                        n, p = divmod(j + 4 - LAG, 4)
                        if p == 0:
                            pe.wait_ge(s_CTl, AHEAD_CT + 8 * (2 * I + n - 1))
                            pe.wait_ge(s_Oe, AHEAD_OE + 2 * I + n - 2)
                        o_part(p, n % 2)
                    with since(pe, I, j, LAG):
                        pe.wait_ge(s_ATl, AHEAD_ATL + SLOTS * I + j + 1 - LAG)
                        pe.wait_ge(s_CTl, AHEAD_CT + 16 * I + 2 * (j - LAG))
                        if (j - LAG) % 4 == 0:
                            pe.wait_ge(s_win[j // 4], 16 * WDMAS * (I + 1))
                        c_part(j)
            last = SLOTS * ITERS
            for j in range(LAG):
                pe.wait_ge(s_ATl, AHEAD_ATL + last + j - LAG)
                transposes(j, last + j + 1 - LAG)
                o_part(4 - LAG + j, 0)
                pe.wait_ge(s_ATl, AHEAD_ATL + last + j + 1 - LAG)
                pe.wait_ge(s_CTl, AHEAD_CT + 2 * (last + j - LAG))
                c_part(j)

            def attn_back(g):
                pe.wait_ge(f_res, g)
                pe.wait_ge(f_stage, g + 1)
                for i in range(TPI):
                    ins = nc.tensor.transpose(bank[0][:, P * i:P * i + P], attnS[:, P * i:P * i + P], ident[:, :])
                ins.then_inc(f_aT, 1)

            def x1_T(g):
                pe.wait_ge(f_xTl, g)
                for i in range(TPI):
                    pe.wait_ge(f_x1, 4 * g + i + 1)
                    ins = nc.tensor.transpose(bank[1][:, P * i:P * i + P], x1[:, i, :], ident[:, :])
                ins.then_inc(f_xT, 1)

            def up(g, i):
                c = slice(P * i, P * i + P)
                pe.wait_ge(f_gelu, AHEAD_GELU + 4 * g + i - 1)
                mm(bank[2 + i % 2][:, :], x1Th[:, c], wuT[:, :], start=True, stop=False)
                mm(bank[2 + i % 2][:, :], x1Tl[:, c], wuT[:, :], start=False, stop=True).then_inc(f_up, 1)

            def h_T(g, i):
                pe.wait_ge(f_gelu, AHEAD_GELU + 4 * g + i + 1)
                pe.wait_ge(f_hTl, AHEAD_HTL + 4 * g + i - 1)
                for k in range(FT):
                    ins = nc.tensor.transpose(bank[4 + i % 2][:, P * k:P * k + P], gS[i % 2][:, P * k:P * k + P], ident[:, :])
                ins.then_inc(f_hT, 1)

            def down(g):
                pe.wait_ge(f_hTl, AHEAD_HTL + 4 * g + 4)
                pe.wait_ge(f_dnE, AHEAD_DNE + g)
                for k in range(FT):
                    mm(bank[6][:, :], wdT[:, k, :], hTh[:, k, :], start=(k == 0), stop=False)
                    ins = mm(bank[6][:, :], wdT[:, k, :], hTl[:, k, :], start=False, stop=(k == FT - 1))
                ins.then_inc(f_dn, 1)

            def down_back(g):
                pe.wait_ge(f_dnE, AHEAD_DNE + g)
                pe.wait_ge(f_y2, AHEAD_Y2 + 4 * g - 4)
                for i in range(TPI):
                    ins = nc.tensor.transpose(bank[7][:, P * i:P * i + P], dS[:, P * i:P * i + P], ident[:, :])
                ins.then_inc(f_back, 1)

            pe.sem_inc(f_hT, AHEAD_HT)
            pe.sem_inc(f_back, AHEAD_BACK)
            attn_back(0)
            pe.wait_ge(s_CTl, AHEAD_CT + 2 * last)
            pe.wait_ge(s_Oe, AHEAD_OE + 2 * ITERS - 1)
            o_part(0, 1)
            o_part(1, 1)
            o_part(2, 1)
            x1_T(0)
            attn_back(1)
            o_part(3, 1)
            pe.wait_ge(f_xTl, 1)
            up(0, 0)
            up(0, 1)
            with pe.Fori(0, ITERS) as g:
                h_T(g, 0)
                up(g, 2)
                with pe.If(g > 0):
                    down_back(g)
                h_T(g, 1)
                up(g, 3)
                h_T(g, 2)
                with pe.If(g < ITERS - 1):
                    x1_T(g + 1)
                h_T(g, 3)
                with pe.If(g < ITERS - 1):
                    pe.wait_ge(f_xTl, g + 2)
                    up(g + 1, 0)
                    up(g + 1, 1)
                with pe.If(g < ITERS - 2):
                    attn_back(g + 2)
                down(g)
            down_back(ITERS)


_INS = ["L0_attn_x", "L0_attn_w_qkv", "L0_attn_w_out", "L0_attn_b_out", "L0_attn_w_th", "L0_ffn_w_up", "L0_ffn_w_down"]


def kernel(**inputs):
    import numpy as np
    import concourse.bacc as bacc
    from concourse.bass_utils import run_bass_kernel_spmd

    nc = bacc.Bacc("TRN2", target_bir_lowering=False, num_devices=1)
    arrays, args = {}, []
    for name in _INS:
        a = np.ascontiguousarray(inputs[name])
        arrays[f"in_{name}"] = a
        args.append(nc.dram_tensor(f"in_{name}", a.shape, mybir.dt.from_np(a.dtype), kind="ExternalInput").ap())
    out = nc.dram_tensor("out", (B, N, D), F32, kind="ExternalOutput").ap()
    x_rows = nc.dram_tensor("x_rows", (ITERS, XROWS, 3 * D), F32, kind="Internal").ap()
    bos_rows = nc.dram_tensor("bos_rows", (ITERS, 3 * D), F32, kind="Internal").ap()
    pt_rows = nc.dram_tensor("pt_rows", (H, P, P), F32, kind="Internal").ap()
    attention_ffn(nc, *args, out, x_rows, bos_rows, pt_rows)
    r = run_bass_kernel_spmd(nc, [arrays], core_ids=[0])
    return r.results[0]["out"]
```
